# Optimizing a Trainium2 kernel written in Bass

```python
import numpy as np
import jax
import jax.numpy as jnp

def _softmax(x, axis=-1):
    return jax.nn.softmax(x, axis=axis)

def _gelu(x):
    return jax.nn.gelu(x, approximate=True)

def _silu(x):
    return jax.nn.silu(x)

def _sigmoid(x):
    return jax.nn.sigmoid(x)

def _layernorm(x, axis=-1, eps=1e-05):
    m = jnp.mean(x, axis=axis, keepdims=True)
    v = jnp.var(x, axis=axis, keepdims=True)
    return (x - m) / jnp.sqrt(v + eps)

def _scatter_add(tgt, idx, src, axis=0):
    return tgt.at[idx].add(src)

def _segment_sum(src, seg, n):
    return jax.ops.segment_sum(src, seg, n)
kernel_name = 'mk_metaformer_d1_conv_nchw512_r2_04bee0'

def setup_inputs(seed: int=0):
    np.random.seed(seed)
    _w = jnp.asarray

    def _rec_inputs():
        import jax
        import jax.numpy as jnp
        _gk = jax.random.key(seed)
        x = 1.508e-05 + 1 * jax.random.normal(jax.random.fold_in(_gk, 1), (8, 256, 64, 64), jnp.float32)
        return x
    x = _rec_inputs()

    def _L0_conv_setup():
        import jax, jax.numpy as jnp
        import numpy as np
        CHANNELS = [256, 128, 64, 32]
        key = jax.random.key(seed)
        x = jax.random.normal(key, (8, 256, 64, 64), dtype=jnp.float32)
        return {'x': x, 'ind': 0}
    _L0_conv_all = _L0_conv_setup()
    _L0_conv_in = {k: v for k, v in _L0_conv_all.items() if k in ()}
    del _L0_conv_all

    def _L0_ffn_setup():
        import jax, jax.numpy as jnp
        import numpy as np
        MARK_AX, OP_ADD, OP_SUB = (0, 1, 2)
        ALU_LO, ALU_HI = (16, 32)
        AX_CARRY_LO, AX_CARRY_HI = (48, 32)
        OPCODE_BASE = 40
        OUTPUT_LO, OUTPUT_HI, CARRY = (64, 72, 80)
        NIB_A, NIB_B, OP_START = (0, 1, 10)
        RESULT, CARRY_OUT = (50, 101)
        GE_POS, GE_DIM = (8, 80)
        OPC_ADD, OPC_SUB = (25, 26)
        B, S, D = (8, 2048, 256)

        def _decode_nibble(x, base):
            return jnp.argmax(x[..., base:base + 16] > 0.5, axis=-1).astype(x.dtype)

        def _pipeline(h, W, b):
            for i in range(3):
                h = jnp.einsum('bspd,od->bspo', h, W[i]) + b[i]
                if i < 2:
                    h = jax.nn.relu(h)
            return h
        key = jax.random.key(seed)
        kx, k1, k2, k3, k4 = jax.random.split(key, 5)
        x_bd = jax.random.uniform(kx, (B, S, D), dtype=jnp.float32)
        Wa = jax.random.normal(k1, (3, GE_DIM, GE_DIM), dtype=jnp.float32) * 0.05
        ba = jax.random.normal(k2, (3, GE_DIM), dtype=jnp.float32) * 0.05
        Ws = jax.random.normal(k3, (3, GE_DIM, GE_DIM), dtype=jnp.float32) * 0.05
        bs = jax.random.normal(k4, (3, GE_DIM), dtype=jnp.float32) * 0.05
        return {'x_bd': x_bd, 'Wa': Wa, 'ba': ba, 'Ws': Ws, 'bs': bs}
    _L0_ffn_all = _L0_ffn_setup()
    _L0_ffn_in = {k: v for k, v in _L0_ffn_all.items() if k in ('Wa', 'ba', 'Ws', 'bs')}
    del _L0_ffn_all
    return {'x': x, 'L0_ffn_Wa': _L0_ffn_in['Wa'], 'L0_ffn_ba': _L0_ffn_in['ba'], 'L0_ffn_Ws': _L0_ffn_in['Ws'], 'L0_ffn_bs': _L0_ffn_in['bs']}

def reference(x, L0_ffn_Wa, L0_ffn_ba, L0_ffn_Ws, L0_ffn_bs):
    import jax
    import jax.numpy as jnp

    def _L0_conv_ref(x, ind):
        import jax, jax.numpy as jnp
        import numpy as np
        CHANNELS = [256, 128, 64, 32]
        C = CHANNELS[ind]
        assert x.shape[1] == C
        kernel = jnp.full((C, 1, 3, 3), 1.0 / 9.0, dtype=x.dtype)
        out = jax.lax.conv_general_dilated(x, kernel, window_strides=(1, 1), padding=((1, 1), (1, 1)), feature_group_count=C, dimension_numbers=('NCHW', 'OIHW', 'NCHW'))
        return out

    def _L0_ffn_ref(x_bd, Wa, ba, Ws, bs):
        import jax, jax.numpy as jnp
        import numpy as np
        MARK_AX, OP_ADD, OP_SUB = (0, 1, 2)
        ALU_LO, ALU_HI = (16, 32)
        AX_CARRY_LO, AX_CARRY_HI = (48, 32)
        OPCODE_BASE = 40
        OUTPUT_LO, OUTPUT_HI, CARRY = (64, 72, 80)
        NIB_A, NIB_B, OP_START = (0, 1, 10)
        RESULT, CARRY_OUT = (50, 101)
        GE_POS, GE_DIM = (8, 80)
        OPC_ADD, OPC_SUB = (25, 26)
        B, S, D = (8, 2048, 256)

        def _decode_nibble(x, base):
            return jnp.argmax(x[..., base:base + 16] > 0.5, axis=-1).astype(x.dtype)

        def _pipeline(h, W, b):
            for i in range(3):
                h = jnp.einsum('bspd,od->bspo', h, W[i]) + b[i]
                if i < 2:
                    h = jax.nn.relu(h)
            return h
        x = x_bd
        Bsz, seq, _ = x.shape
        x_ge = jnp.zeros((Bsz, seq, GE_POS, GE_DIM), dtype=x.dtype)
        x_ge = x_ge.at[..., 0, NIB_A].set(_decode_nibble(x, ALU_LO))
        x_ge = x_ge.at[..., 1, NIB_A].set(_decode_nibble(x, ALU_HI))
        x_ge = x_ge.at[..., 0, NIB_B].set(_decode_nibble(x, AX_CARRY_LO))
        x_ge = x_ge.at[..., 1, NIB_B].set(_decode_nibble(x, AX_CARRY_HI))
        x_ge = x_ge.at[..., :, OP_START + OPC_ADD].set(x[..., OPCODE_BASE + OPC_ADD][..., None])
        x_ge = x_ge.at[..., :, OP_START + OPC_SUB].set(x[..., OPCODE_BASE + OPC_SUB][..., None])
        mark = x[..., MARK_AX] > 0.5
        m_add = mark & (x[..., OP_ADD] > 0.5)
        m_sub = mark & ~(x[..., OP_ADD] > 0.5) & (x[..., OP_SUB] > 0.5)
        active = (m_add | m_sub).astype(x.dtype)
        y_add = _pipeline(x_ge, Wa, ba)
        y_sub = _pipeline(x_ge, Ws, bs)
        y = jnp.where(m_add[..., None, None], y_add, jnp.where(m_sub[..., None, None], y_sub, x_ge))
        res_lo = jnp.clip(jnp.round(y[..., 0, RESULT]), 0, 15).astype(jnp.int32)
        res_hi = jnp.clip(jnp.round(y[..., 1, RESULT]), 0, 15).astype(jnp.int32)
        oh_lo = jax.nn.one_hot(res_lo, 16, dtype=x.dtype) * active[..., None]
        oh_hi = jax.nn.one_hot(res_hi, 16, dtype=x.dtype) * active[..., None]
        carry = (jnp.round(y[..., 1, CARRY_OUT]) > 0.5).astype(x.dtype) * active
        out = x
        out = out.at[..., OUTPUT_LO:OUTPUT_LO + 16].add(2.0 * oh_lo)
        out = out.at[..., OUTPUT_HI:OUTPUT_HI + 16].add(2.0 * oh_hi)
        out = out.at[..., CARRY].add(carry)
        return out

    def _gn(v, G=32, eps=1e-05):
        B_, C_, H_, W_ = v.shape
        g = v.reshape(B_, G, C_ // G, H_, W_)
        m = jnp.mean(g, axis=(2, 3, 4), keepdims=True)
        s = jnp.var(g, axis=(2, 3, 4), keepdims=True)
        return ((g - m) / jnp.sqrt(s + eps)).reshape(v.shape)

    def _ln_c(v, eps=1e-06):
        m = jnp.mean(v, axis=1, keepdims=True)
        s = jnp.var(v, axis=1, keepdims=True)
        return (v - m) / jnp.sqrt(s + eps)

    def _ln_t(v, eps=1e-05):
        m = jnp.mean(v, axis=-1, keepdims=True)
        s = jnp.var(v, axis=-1, keepdims=True)
        return (v - m) / jnp.sqrt(s + eps)

    def _to_tokens(v):
        B_, C_, H_, W_ = v.shape
        return v.reshape(B_, C_, H_ * W_).transpose(0, 2, 1)

    def _from_tokens(t, like):
        B_, C_, H_, W_ = like.shape
        return t.transpose(0, 2, 1).reshape(B_, C_, H_, W_)
    x = x + _L0_conv_ref(_ln_c(x), 0)
    t = _to_tokens(x)
    t = t + _L0_ffn_ref(_ln_t(t), L0_ffn_Wa, L0_ffn_ba, L0_ffn_Ws, L0_ffn_bs)
    x = _from_tokens(t, x)
    return x

_drawn_inputs = setup_inputs


def setup_inputs(seed=0):
    import zlib

    import numpy as np

    out = dict(_drawn_inputs(seed))
    spreads = {}
    factors = {}
    for name, (base, spread) in spreads.items():
        noise = np.random.default_rng([zlib.crc32(name.encode()), seed]).standard_normal(out[name].shape)
        drawn = base * np.exp(spread * noise) if base else spread * noise
        out[name] = jnp.asarray(drawn.astype(out[name].dtype))
    for name, factor in factors.items():
        out[name] = (out[name] * factor).astype(out[name].dtype)
    return out
```

```python
from contextlib import ExitStack

import concourse.bass as bass
from concourse import mybir

F32 = mybir.dt.float32
F32R = mybir.dt.float32r
F16 = mybir.dt.float16
BF16 = mybir.dt.bfloat16
ALU = mybir.AluOpType
ACT = mybir.ActivationFunctionType

B, C, H, W = 8, 256, 64, 64
P = 128
D = 80
IMGS = P // H
PAIRS = B // IMGS
CW = 8
CHUNKS = W // CW
NCHUNK = PAIRS * CHUNKS
HALF = CW // 2
RING = 32
GROUPS = CW // 2
QC = 4

ALU_LO, ALU_HI, AX_LO, OP_COL, OUT_LO, OUT_HI, CARRY = 16, 32, 48, 65, 64, 72, 80
NIB = 16
UC = OP_COL + 2
OP_ADD_F = 35
RESULT = 50
CARRY_F = D - 1
MAIN = P - D
REM = D - MAIN

NV = 11
V_LO, V_HI, V_ONE = 6, 8, 10
PARTS = 3
ROWS = 2 * PARTS * NV

SCALE = 2048.0
MAGIC = 1.5 * 2.0 ** 23

K_ID, K_BAND, K_RANK, K_IOTA, K_ISA, K_ISS, K_T80, K_T81, K_EPS = 0, 128, 256, 304, 320, 321, 322, 323, 324
K_N = K_EPS + 2 * CW

B_CONV, B_L1M, B_L1R, B_L2, B_FT, B_Y, B_YT = 0, 2, 3, 4, 5, 6, 7

LAST_STEP = NCHUNK + 6


class Chain:

    def __init__(self, eng, sem, per):
        self.eng, self.sem, self.per, self.n = eng, sem, per, 0

    def resume(self, i, n):
        self.base, self.n = i * self.per, n

    def turn(self, i):
        self.resume(i, 0)
        if not isinstance(i, int) or i > 0:
            self.eng.wait_ge(self.sem, self.base)

    def done(self, ins):
        ins.then_inc(self.sem, 1)
        self.n += 1
        self.eng.wait_ge(self.sem, self.base + self.n)

    def end(self):
        assert self.n == self.per, (self.n, self.per)


def known(i):
    return isinstance(i, int)


def wait(eng, sem, value):
    if not known(value) or value > 0:
        eng.wait_ge(sem, value)


def chunk_at(t, j, pair, lag):
    c = t - lag
    if known(c) and not 0 <= c < NCHUNK:
        return None
    behind = 1 if lag > j else 0
    return c, (j - lag) % CHUNKS, (pair + behind) % 2


def run_steps(eng, step):
    for t in range(CHUNKS):
        step(t, t, 0)
    with eng.Fori(1, PAIRS) as pair:
        for j in range(CHUNKS):
            with eng.register(f"pair_{eng.engine.name}_{j}") as copy:
                eng.reg_mov(copy, pair)
                here = eng.snap(copy, min_val=1, max_val=PAIRS - 1)
                step(here * CHUNKS + j, j, here)
    for t in range(NCHUNK, LAST_STEP):
        step(t, t % CHUNKS, t // CHUNKS)


def build(nc, x_d, wa_d, ba_d, ws_d, bs_d, cst_d, out_d):
    with ExitStack() as ctx:
        def sb(name, shape, dt):
            return ctx.enter_context(nc.sbuf_tensor(name, shape, dt))

        def sem(name):
            return ctx.enter_context(nc.semaphore(name))

        xbuf = sb("xbuf", [P, 2 * C * W], F32)
        n32 = sb("n32", [P, 2, HALF, C], F32)
        nhi = sb("nhi", [P, RING, C], F16)
        nlo = sb("nlo", [P, RING, C], F16)
        cst = sb("consts", [P, K_N], F32)
        band = sb("band", [P, P], F16)
        identb = sb("identb", [P, P], BF16)
        stat = sb("stat", [P, 2 * CW, 6], F32)
        s_sum = sb("s_sum", [P, 2 * CW], F32)
        s_dif = sb("s_dif", [P, 2 * CW], F32)
        s_m2 = sb("s_m2", [P, 2 * CW], F32)
        s_dd = sb("s_dd", [P, 2 * CW], F32)
        s_var = sb("s_var", [P, 2, 2 * CW], F32)
        s_sqrt = sb("s_sqrt", [P, 2, 2 * CW], F32)
        s_r0 = sb("s_r0", [P, 2 * CW], F32)
        s_nt = sb("s_nt", [P, 2 * CW], F32)
        s_nu = sb("s_nu", [P, 2 * CW], F32)
        mean = sb("mean", [P, 4, 2 * CW], F32)
        rstd = sb("rstd", [P, 4, 2 * CW], F32)
        rn = sb("rn", [P, 4, CW], F32)
        gain = sb("gain", [P, 4, CW], F32)
        shift = sb("shift", [P, 4, CW], F32)
        ut = sb("ut", [P, CW, UC], F32)
        u = sb("u", [P, CW, UC], F32)
        g = sb("g", [P, CW, 3 * NIB], F32)
        gw = sb("gw", [P, CW, 3, NIB], F32)
        mx1 = sb("mx1", [P, CW, 3], F32)
        nfree = sb("nfree", [P, CW, 3], F32)
        nhit = sb("nhit", [P, CW, 3], F32)
        marks = sb("marks", [P, CW, 3], F32)
        noadd = sb("noadd", [P, CW], F32)
        subraw = sb("subraw", [P, CW], F32)
        xres = sb("xres", [P, CW, 2], F32)
        msk = sb("msk", [P, 4, 3, CW], F32)
        val = sb("val", [P, CW, NV], BF16)
        feat = sb("feat", [P, 2, CW, P], BF16)
        featT = sb("featT", [P, 2, 2, 4 * P], BF16)
        h1m = sb("h1m", [P, 2, 512], F32)
        h1r = sb("h1r", [P, 2, 512], F32R)
        h2 = sb("h2", [P, 2, 512], F32)
        ysb = sb("ysb", [P, 512], F32)
        ya = sb("ya", [P, CW, 2, 2], F32)
        ys = sb("ys", [P, CW, 2, 2], F32)
        yy = sb("yy", [P, CW, 2, 2], F32)
        yc = sb("yc", [P, CW, 2], F32)
        yr = sb("yr", [P, CW, 2], F32)
        yrr = sb("yrr", [P, CW, 2], F32)
        ycar = sb("ycar", [P, CW], F32)
        ycar2 = sb("ycar2", [P, CW], F32)
        hot = sb("hot", [P, CW, 2, NIB], F32)
        raw = nlo[:, :, :].rearrange("p s c -> p (s c)").bitcast(F32)
        nat = raw[:, 0:2 * D].rearrange("p (k d) -> p k d", k=2)
        nat2, nat2r, nat3 = (raw[:, (2 + k) * P:(3 + k) * P] for k in range(3))
        tl = raw[:, 5 * P:5 * P + 5 * P // 2].bitcast(BF16) \
            .rearrange("p (k n) -> p k n", k=5)
        natb = sb("natb", [P, 2], F32)
        b2 = sb("b2", [P, 2], F32)
        base, res, res2 = (raw[:, k * P:k * P + 3 * NV].rearrange("p (k v) -> p k v", k=3) for k in (8, 9, 10))
        part = sb("part", [P, 3, PARTS, NV], BF16)
        w1 = sb("w1", [P, 5, P], BF16)
        w2m = sb("w2m", [P, P], F32)
        w2r = sb("w2r", [P, P], F32R)
        w3 = sb("w3", [P, 32], F32)

        ps = ctx.enter_context(nc.psum_tensor("ps", [P, 8, 512], F32))
        ftp = ps[:, B_FT, :].bitcast(BF16)
        ytv = ps[:, B_YT, :].rearrange("p (b m o) -> p b m o", b=CW, m=2)

        cst_loaded = sem("cst_loaded")
        w_loaded = sem("w_loaded")
        zeroed = sem("zeroed")
        setup_v = sem("setup_v")
        setup_pe = sem("setup_pe")
        x_loaded = sem("x_loaded")
        stored = [sem(f"stored{q}") for q in range(QC)]
        ln = sem("ln")
        var_ready = sem("var_ready")
        sqrt_ready = sem("sqrt_ready")
        fin_ready = sem("fin_ready")
        n_ready = sem("n_ready")
        hi_ready = sem("hi_ready")
        lo_ready = sem("lo_ready")
        conv_done = sem("conv_done")
        x1_done = sem("x1_done")
        u_read = sem("u_read")
        dec = sem("dec")
        rank_ready = sem("rank_ready")
        top_ready = sem("top_ready")
        feat_ready = sem("feat_ready")
        ft_done = sem("ft_done")
        ft_copied = sem("ft_copied")
        l1m_done = sem("l1m_done")
        l1r_done = sem("l1r_done")
        h1m_ready = sem("h1m_ready")
        h1hi_ready = sem("h1hi_ready")
        h1lo_ready = sem("h1lo_ready")
        l2_done = sem("l2_done")
        h2_ready = sem("h2_ready")
        l3_done = sem("l3_done")
        y_copied = sem("y_copied")
        yt_done = sem("yt_done")
        y_read = sem("y_read")
        out_ready = sem("out_ready")
        hotc = sem("hotc")

        def xview(parity):
            lo = parity * (C * W)
            return xbuf[:, bass.ds(lo, C * W)].rearrange("p (c w) -> p w c", w=W)

        def over(ap, shape):
            return ap.broadcast_to(shape)

        block = ctx.enter_context(nc.Block())

        @block.sync
        def _(sp):
            def tile_part(parity, img, q):
                n = C // QC * W
                return xbuf[img * H:(img + 1) * H, bass.ds(parity * (C * W) + q * n, n)] \
                    .rearrange("p (c w) -> p c w", w=W)

            def dram_part(ap, pair, img, q):
                cs = slice(q * (C // QC), (q + 1) * (C // QC))
                return ap[bass.ds(pair * IMGS + img, 1), cs].rearrange("b c h w -> (b h) c w")

            def load(pair, parity, q):
                for img in range(IMGS):
                    sp.dma_start(tile_part(parity, img, q), dram_part(x_d, pair, img, q)).then_inc(x_loaded, 16)

            def store(pair, q):
                for img in range(IMGS):
                    sp.dma_start(dram_part(out_d, pair, img, q), tile_part(pair % 2, img, q)) \
                        .then_inc(stored[q], 16)

            per_pair = 16 * IMGS * QC
            sp.dma_start(cst[:, :], cst_d).then_inc(cst_loaded, 16)
            for q in range(QC):
                load(0, 0, q)
            sp.wait_ge(x_loaded, per_pair)
            for q in range(QC):
                load(1, 1, q)
            with sp.Fori(0, PAIRS - 2) as pair:
                sp.wait_ge(x_loaded, per_pair * (pair + 2))
                sp.wait_ge(hotc, (pair + 1) * (CHUNKS * HOT_STEPS))
                for q in range(QC):
                    store(pair, q)
                for q in range(QC):
                    sp.wait_ge(stored[q], 16 * IMGS * (pair + 1))
                    load(pair + 2, pair % 2, q)
            with sp.Fori(PAIRS - 2, PAIRS) as pair:
                sp.wait_ge(hotc, (pair + 1) * (CHUNKS * HOT_STEPS))
                for q in range(QC):
                    store(pair, q)
            for q in range(QC):
                sp.wait_ge(stored[q], 16 * IMGS * PAIRS)

        @block.vector
        def _(v):
            v.memset(nat2[:, :], 0.0)
            v.memset(nat2r[:, :], 0.0)
            v.memset(nat3[:, :], 0.0)
            v.memset(b2[:, :], 0.0)
            v.memset(base[:, :, :], 0.0).then_inc(zeroed, 1)
            v.memset(tl[:, :, :], 0.0)
            v.memset(feat[:, :, :, :], 0.0)
            v.memset(stat[:, :, :], 0.0)
            v.memset(val[:, :, V_ONE:V_ONE + 1], 1.0).then_inc(zeroed, 1)
            n_setup = [0]

            def done(ins):
                n_setup[0] += 1
                ins.then_inc(setup_v, 1)
                v.wait_ge(setup_v, n_setup[0])

            v.wait_ge(zeroed, 2)
            v.wait_ge(cst_loaded, 16)
            v.tensor_copy(identb[:, :], cst[:, K_ID:K_ID + P])
            v.tensor_copy(band[:, :], cst[:, K_BAND:K_BAND + P])
            v.wait_ge(w_loaded, W_DMAS * 16)
            for k in range(2):
                for j in range(PARTS):
                    v.tensor_copy(base[:, k, 2 * j:2 * j + 2], nat[:, k, OP_ADD_F:OP_ADD_F + 2])
                for at in (V_LO, V_HI):
                    v.tensor_copy(base[:, k, at:at + 2], nat[:, k, 0:2])
                v.tensor_copy(base[:, k, V_ONE:V_ONE + 1], natb[:, k:k + 1])
            done(v.tensor_copy(base[:, 2, 0:2], b2[:, :]))
            done(v.tensor_copy(part[:, :, 0, :], base[:, :, :]))
            done(v.tensor_tensor(res[:, :, :], base[:, :, :], part[:, :, 0, :], ALU.subtract))
            done(v.tensor_copy(part[:, :, 1, :], res[:, :, :]))
            done(v.tensor_tensor(res2[:, :, :], res[:, :, :], part[:, :, 1, :], ALU.subtract))
            done(v.tensor_copy(part[:, :, 2, :], res2[:, :, :]))
            flat = part[:, :, :, :].rearrange("p k j v -> p k (j v)")
            half = PARTS * NV
            for pos in range(2):
                v.tensor_scalar(tl[:, pos, 0:half], flat[:, 0, :], cst[:, K_ISA:K_ISA + 1], None, ALU.mult)
                v.tensor_scalar(tl[:, pos, half:2 * half], flat[:, 0, :], cst[:, K_ISS:K_ISS + 1], None, ALU.mult)
                v.tensor_copy(tl[:, 2 + pos, half:2 * half], flat[:, 1, :])
            for m in range(2):
                for j in range(PARTS):
                    at = (m * PARTS + j) * NV + V_ONE
                    if j == 0:
                        one = K_T80 if m == 0 else K_T81
                        ins = v.tensor_tensor(tl[:, 4, at:at + 1], part[:, 2, j, m:m + 1], cst[:, one:one + 1],
                                              ALU.add)
                    else:
                        ins = v.tensor_copy(tl[:, 4, at:at + 1], part[:, 2, j, m:m + 1])
            done(ins)
            for k in range(4):
                at = V_HI if k % 2 == 0 else V_LO
                rows = tl[:, k, 0:ROWS].rearrange("p (r v) -> p r v", v=NV)
                ins = v.memset(rows[:, :, at:at + 2], 0.0)
            done(ins)
            v.wait_ge(setup_pe, 1)
            v.tensor_copy(w1[:, :, :], ftp[:, 0:5 * P].rearrange("p (k n) -> p k n", k=5))
            wt = ps[:, B_YT, :].rearrange("p (k n) -> p k n", k=4)
            v.tensor_copy(w2m[:, :], wt[:, 0, :])
            v.tensor_copy(w3[:, :], wt[:, 2, 0:32])
            done(v.tensor_copy(w2r[:, :], wt[:, 1, :]))
            for q in (1, 3):
                rows = slice(32 * q, 32 * q + 32)
                ins = v.tensor_tensor(w2r[rows, :], wt[rows, 1, :], w2r[rows, :], ALU.subtract)
            done(ins)
            assert n_setup[0] == SETUP_V

            lnc = Chain(v, ln, LN_STEPS)
            hc = Chain(v, hotc, HOT_STEPS)

            def step(t, j, pair):
                slot = j % 4
                first = chunk_at(t, j, pair, 0)
                norm = chunk_at(t, j, pair, 1)
                conv = chunk_at(t, j, pair, 2)
                tok = chunk_at(t, j, pair, 3)
                last = chunk_at(t, j, pair, 6)
                if not known(t) or 1 <= t <= NCHUNK + 2:
                    k = (slot - 1) % 4
                    i = (j - 1) % 2
                    lnc.resume(t - 1, AGG_STEPS)
                    v.wait_ge(sqrt_ready, t)
                    lnc.done(v.reciprocal(s_r0[:, :], s_sqrt[:, i, :]))
                    lnc.done(v.scalar_tensor_tensor(s_nt[:, :], s_r0[:, :], -0.5, s_r0[:, :], ALU.mult, ALU.mult))
                    lnc.done(v.tensor_tensor(s_nu[:, :], s_nt[:, :], s_var[:, i, :], ALU.mult))
                    lnc.done(v.scalar_tensor_tensor(rstd[:, k, :], s_nu[:, :], 1.5, s_r0[:, :], ALU.add, ALU.mult))
                    lnc.end()
                    v.tensor_scalar(rn[:, k, :], rstd[:, k, 0:CW], SCALE / 9.0, None, ALU.mult)
                    v.tensor_scalar(gain[:, k, :], rstd[:, k, CW:], 1.0, None, ALU.add)
                    v.scalar_tensor_tensor(shift[:, k, :], mean[:, k, CW:], -1.0, rstd[:, k, CW:],
                                           ALU.mult, ALU.mult).then_inc(fin_ready, 1)
                    v.wait_ge(fin_ready, t)

                def normalise(h):
                    c, jc, par = norm
                    xv = xview(par)
                    wait(v, lo_ready, 2 * c + h - 1)
                    for i in range(HALF):
                        w = h * HALF + i
                        ins = v.tensor_scalar(n32[:, h, i, :], xv[:, jc * CW + w, :],
                                              mean[:, (slot - 1) % 4, w:w + 1], rn[:, (slot - 1) % 4, w:w + 1],
                                              ALU.subtract, ALU.mult)
                    ins.then_inc(n_ready, 1)

                def x1_statistics(s):
                    c, jc, par = conv
                    for i in (2 * s, 2 * s + 1):
                        ins = v.bn_stats(stat[:, CW + i, :], xview(par)[:, jc * CW + i, :])
                    return ins

                for s in range(GROUPS):
                    if conv and s > 0:
                        v.wait_ge(x1_done, 4 * conv[0] + s)
                    tau = 4 * (t - 4) + s - 1
                    if not known(tau) or 0 <= tau < 4 * NCHUNK:
                        low = h1r[64:, (s - 1) % 2, :]
                        v.wait_ge(h1hi_ready, tau + 1)
                        v.scalar_tensor_tensor(low, ps[64:, B_L1R, :], 0.0, low,
                                               ALU.max, ALU.subtract).then_inc(h1lo_ready, 1)
                    if conv and s > 0:
                        x1_statistics(s - 1)
                    if s == 0 and last:
                        results(last, (slot - 6) % 4)
                    if norm and s < 2:
                        normalise(s)
                    if first and j == 0 and s == 0:
                        v.wait_ge(x_loaded, (pair + 1) * 16 * IMGS * QC)
                    if conv:
                        c, jc, par = conv
                        w = jc * CW + 2 * s
                        pair_cols = xview(par)[:, w:w + 2, :]
                        v.wait_ge(conv_done, 4 * c + s + 1)
                        v.tensor_tensor(pair_cols, ps[:, B_CONV + s % 2, :].rearrange("p (w c) -> p w c", w=2),
                                        pair_cols, ALU.add).then_inc(x1_done, 1)
                    if first:
                        c, jc, par = first
                        for i in (2 * s, 2 * s + 1):
                            counted = v.bn_stats(stat[:, i, :], xview(par)[:, jc * CW + i, :])
                if conv:
                    v.wait_ge(x1_done, 4 * conv[0] + 4)
                if tok:
                    v.wait_ge(rank_ready, tok[0] + 1)
                    v.tensor_reduce(mx1[:, :, :], gw[:, :, :, :], mybir.AxisListType.X,
                                    ALU.max).then_inc(top_ready, 1)
                if conv:
                    counted = x1_statistics(GROUPS - 1)
                if not known(t) or t <= NCHUNK + 1:
                    lnc.resume(t, 0)
                    lnc.done(counted)
                    wait(v, out_ready, t - 5)
                    v.tensor_tensor(s_sum[:, :], stat[:, :, 1], stat[:, :, 4], ALU.add)
                    v.tensor_tensor(s_dif[:, :], stat[:, :, 1], stat[:, :, 4], ALU.subtract)
                    lnc.done(v.tensor_tensor(s_m2[:, :], stat[:, :, 2], stat[:, :, 5], ALU.add))
                    v.tensor_scalar(mean[:, slot, :], s_sum[:, :], 0.5, None, ALU.mult)
                    v.scalar_tensor_tensor(s_dd[:, :], s_dif[:, :], 0.25, s_dif[:, :], ALU.mult, ALU.mult)
                    lnc.done(v.scalar_tensor_tensor(s_m2[:, :], s_m2[:, :], 1.0 / C, cst[:, K_EPS:K_EPS + 2 * CW],
                                                    ALU.mult, ALU.add))
                    lnc.done(v.tensor_tensor(s_var[:, j % 2, :], s_m2[:, :], s_dd[:, :], ALU.add))

            def results(last, k):
                c, jc, par = last
                cols = xview(par)[:, jc * CW:(jc + 1) * CW, :]
                hc.turn(c)
                v.wait_ge(yt_done, c + 1)
                v.wait_ge(feat_ready, c + 1)
                v.wait_ge(out_ready, c + 1)
                four = [P, CW, 2, 2]
                add, sub, act = (msk[:, k, i, :] for i in range(3))
                v.tensor_tensor(ya[:, :, :, :], ytv[:, :, :, 0:2], over(add.unsqueeze(2).unsqueeze(3), four),
                                ALU.mult)
                v.tensor_tensor(ys[:, :, :, :], ytv[:, :, :, 2:4], over(sub.unsqueeze(2).unsqueeze(3), four),
                                ALU.mult).then_inc(y_read, 1)
                v.wait_ge(y_read, c + 1)
                hc.done(v.tensor_tensor(yy[:, :, :, :], ya[:, :, :, :], ys[:, :, :, :], ALU.add))
                v.tensor_scalar(ycar[:, :], yy[:, :, 1, 1], 0.5, None, ALU.is_gt)
                hc.done(v.tensor_scalar(yc[:, :, :], yy[:, :, :, 0], 0.0, float(NIB - 1), ALU.max, ALU.min))
                v.tensor_tensor(ycar2[:, :], ycar[:, :], act, ALU.mult)
                hc.done(v.tensor_scalar(yr[:, :, :], yc[:, :, :], MAGIC, MAGIC, ALU.add, ALU.subtract))
                hc.done(v.scalar_tensor_tensor(yrr[:, :, :], yr[:, :, :], 1.0,
                                               over(act.unsqueeze(2), [P, CW, 2]), ALU.add, ALU.mult))
                hot_shape = [P, CW, 2, NIB]
                hc.done(v.tensor_tensor(hot[:, :, :, :],
                                        over(cst[:, K_IOTA:K_IOTA + NIB].unsqueeze(1).unsqueeze(2), hot_shape),
                                        over(yrr[:, :, :].unsqueeze(3), hot_shape), ALU.is_equal))
                for i, at in enumerate((OUT_LO, OUT_HI)):
                    hc.done(v.scalar_tensor_tensor(cols[:, :, at:at + NIB], hot[:, :, i, :], 2.0,
                                                   cols[:, :, at:at + NIB], ALU.mult, ALU.add))
                hc.done(v.tensor_tensor(cols[:, :, CARRY], cols[:, :, CARRY], ycar2[:, :], ALU.add))
                hc.end()

            run_steps(v, step)

        @block.gpsimd
        def _(pool):
            dc = Chain(pool, dec, DEC_STEPS)

            def step(t, j, pair):
                norm = chunk_at(t, j, pair, 1)
                tok = chunk_at(t, j, pair, 3)
                k4 = (j - 3) % 4

                def low_parts(h):
                    c, jc, par = norm
                    at = (jc * CW + h * HALF) % RING
                    pool.wait_ge(hi_ready, 2 * c + h + 1)
                    pool.tensor_tensor(nlo[:, at:at + HALF, :], n32[:, h, :, :], nhi[:, at:at + HALF, :],
                                       ALU.subtract).then_inc(lo_ready, 1)

                if tok:
                    c, jc, par = tok
                    dc.turn(c)
                    pool.wait_ge(fin_ready, t)
                    shape = [P, CW, UC]
                    dc.done(pool.tensor_tensor(ut[:, :, :], xview(par)[:, jc * CW:(jc + 1) * CW, 0:UC],
                                               over(mean[:, (j - 1) % 4, CW:].unsqueeze(2), shape), ALU.subtract))
                    pool.tensor_tensor(u[:, :, :], ut[:, :, :],
                                       over(rstd[:, (j - 1) % 4, CW:].unsqueeze(2), shape),
                                       ALU.mult).then_inc(u_read, 1)
                    pool.wait_ge(u_read, c + 1)
                    wait(pool, hotc, (c - 3) * HOT_STEPS)
                if norm:
                    low_parts(0)
                if tok:
                    if known(c) and c == 0:
                        pool.wait_ge(zeroed, 2)
                        pool.wait_ge(cst_loaded, 16)
                    add, sub, act = (msk[:, k4, i, :] for i in range(3))
                    pool.tensor_scalar(g[:, :, :], u[:, :, ALU_LO:ALU_LO + 3 * NIB], 0.5, None, ALU.is_gt)
                    pool.tensor_scalar(marks[:, :, :], u[:, :, 0:3], 0.5, None, ALU.is_gt)
                    dc.done(pool.tensor_copy(val[:, :, 0:2], u[:, :, OP_COL:OP_COL + 2]))
                    rank = cst[:, K_RANK:K_RANK + 3 * NIB]
                    pool.tensor_tensor(gw[:, :, :, :].rearrange("p b k n -> p b (k n)"), g[:, :, :],
                                       over(rank.unsqueeze(1), [P, CW, 3 * NIB]), ALU.mult).then_inc(rank_ready, 1)
                    pool.tensor_tensor(add, marks[:, :, 0], marks[:, :, 1], ALU.mult)
                    pool.tensor_tensor(subraw[:, :], marks[:, :, 0], marks[:, :, 2], ALU.mult)
                    pool.tensor_scalar(noadd[:, :], marks[:, :, 1], -1.0, 1.0, ALU.mult, ALU.add)
                    dc.done(pool.tensor_tensor(xres[:, :, :], u[:, :, OP_COL:OP_COL + 2], val[:, :, 0:2],
                                               ALU.subtract))
                    pool.tensor_tensor(sub, subraw[:, :], noadd[:, :], ALU.mult)
                    dc.done(pool.tensor_copy(val[:, :, 2:4], xres[:, :, :]))
                    pool.tensor_tensor(act, add, sub, ALU.add)
                    dc.done(pool.tensor_tensor(val[:, :, 4:6], xres[:, :, :], val[:, :, 2:4], ALU.subtract))
                if norm:
                    low_parts(1)
                if tok:
                    c = tok[0]
                    pool.wait_ge(top_ready, c + 1)
                    pool.tensor_tensor(nfree[:, :, :], over(rank[:, 0:1].unsqueeze(1), [P, CW, 3]), mx1[:, :, :],
                                       ALU.subtract)
                    dc.done(pool.tensor_scalar(nhit[:, :, :], mx1[:, :, :], 0.5, None, ALU.is_gt))
                    pool.tensor_tensor(val[:, :, V_LO:V_LO + 2], nfree[:, :, 0:3:2], nhit[:, :, 0:3:2], ALU.mult)
                    dc.done(pool.tensor_tensor(val[:, :, V_HI:V_HI + 2],
                                               over(nfree[:, :, 1:2], [P, CW, 2]),
                                               over(nhit[:, :, 1:2], [P, CW, 2]), ALU.mult))
                    wait(pool, ft_done, c - 1)
                    half = PARTS * NV
                    shape = [P, CW, PARTS, NV]
                    for m, mask in enumerate((add, sub)):
                        ins = pool.tensor_tensor(
                            feat[:, (j + 1) % 2, :, m * half:(m + 1) * half].rearrange("p b (j v) -> p b j v", v=NV),
                            over(val[:, :, :].unsqueeze(2), shape), over(mask.unsqueeze(2).unsqueeze(3), shape),
                            ALU.mult)
                    ins.then_inc(feat_ready, 1)
                    dc.end()
                    pool.wait_ge(feat_ready, c + 1)

            run_steps(pool, step)

        @block.scalar
        def _(act):
            act.wait_ge(zeroed, 1)
            loads = [
                (nat[0:D, 0, :], wa_d[0]), (nat[D:P, 0, :], ws_d[0, 0:MAIN]),
                (nat2[0:D, 0:D], wa_d[1]), (nat2[0:D, D:P], ws_d[1, :, 0:MAIN]),
                (natb[0:D, 0:1], ba_d[0].unsqueeze(1)), (natb[D:P, 0:1], bs_d[0, 0:MAIN].unsqueeze(1)),
                (b2[0:D, 0:1], ba_d[1].unsqueeze(1)), (b2[0:D, 1:2], bs_d[1].unsqueeze(1)),
            ]
            for q in range(4):
                rows = slice(REM * q, REM * (q + 1))
                loads += [(nat[rows, 1, :], ws_d[0, MAIN:D]), (nat2r[0:D, rows], ws_d[1, :, MAIN:D]),
                          (natb[rows, 1:2], bs_d[0, MAIN:D].unsqueeze(1))]
            for i, (w_d, b_d, f) in enumerate(((wa_d, ba_d, RESULT), (wa_d, ba_d, CARRY_F),
                                               (ws_d, bs_d, RESULT), (ws_d, bs_d, CARRY_F))):
                at = D + i // 2
                loads += [(nat3[i:i + 1, 0:D], w_d[2, f:f + 1]), (nat3[i:i + 1, at:at + 1], b_d[2:3, f:f + 1])]
            assert len(loads) == W_DMAS
            for dst, src in loads:
                act.dma_start(dst, src).then_inc(w_loaded, 16)

            def step(t, j, pair):
                norm = chunk_at(t, j, pair, 1)
                tok = chunk_at(t, j, pair, 3)
                ffn = chunk_at(t, j, pair, 4)
                back = chunk_at(t, j, pair, 5)
                for s in range(GROUPS):
                    if s == 0 and ffn:
                        c = ffn[0]
                        act.wait_ge(ft_done, c + 1)
                        wait(act, l2_done, 4 * c - 4)
                        act.activation(featT[:, j % 2, :, :].rearrange("p a n -> p (a n)"), ftp,
                                       ACT.Copy).then_inc(ft_copied, 1)
                    tau = 4 * (t - 4) + s - 1
                    if not known(tau) or 0 <= tau < 4 * NCHUNK:
                        act.wait_ge(l2_done, tau + 1)
                        wait(act, l3_done, tau - 1)
                        act.activation(h2[:, (s - 1) % 2, :], ps[:, B_L2, :], ACT.Relu).then_inc(h2_ready, 1)
                    if norm and s < 2:
                        c, jc, par = norm
                        at = (jc * CW + s * HALF) % RING
                        act.wait_ge(n_ready, 2 * c + s + 1)
                        wait(act, conv_done, 2 * (2 * c + s) - 13)
                        act.activation(nhi[:, at:at + HALF, :], n32[:, s, :, :], ACT.Copy).then_inc(hi_ready, 1)
                    if s == 2 and back:
                        c = back[0]
                        act.wait_ge(l3_done, 4 * c + 4)
                        wait(act, yt_done, c)
                        act.activation(ysb[:, :], ps[:, B_Y, :], ACT.Copy).then_inc(y_copied, 1)
                    if ffn:
                        tau = 4 * ffn[0] + s
                        act.wait_ge(l1m_done, tau + 1)
                        wait(act, l2_done, tau - 1)
                        act.activation(h1m[:, s % 2, :], ps[:, B_L1M, :], ACT.Relu).then_inc(h1m_ready, 1)
                        act.wait_ge(l1r_done, tau + 1)
                        act.activation(h1r[:, s % 2, :], ps[:, B_L1R, :], ACT.Relu).then_inc(h1hi_ready, 1)
                    if tok and s > 0:
                        c, jc, par = tok
                        if s == 1:
                            act.wait_ge(u_read, c + 1)
                        k = (j - 1) % 4
                        for w in range(*((0, 3), (3, 6), (6, 8))[s - 1]):
                            col = xview(par)[:, jc * CW + w, :]
                            ins = act.activation(col, col, ACT.Identity, bias=shift[:, k, w:w + 1],
                                                 scale=gain[:, k, w:w + 1])
                        if s == 3:
                            ins.then_inc(out_ready, 1)
                if not known(t) or t <= NCHUNK + 1:
                    act.wait_ge(ln, LN_STEPS * t + AGG_STEPS)
                    act.activation(s_sqrt[:, j % 2, :], s_var[:, j % 2, :], ACT.Sqrt).then_inc(sqrt_ready, 1)

            run_steps(act, step)

        @block.tensor
        def _(pe):
            pe.wait_ge(setup_v, SETUP_V - 2)
            ident = cst[:, K_ID:K_ID + P]
            for k in range(5):
                pe.transpose(ftp[:, k * P:(k + 1) * P], tl[:, k, :], identb[:, :])
            for k, src in enumerate((nat2, nat2r, nat3)):
                ins = pe.transpose(ps[:, B_YT, k * P:(k + 1) * P], src[:, :], ident)
            ins.then_inc(setup_pe, 1)
            pe.wait_ge(setup_v, SETUP_V)

            def convolve(conv, s):
                c, jc, par = conv
                w = jc * CW + 2 * s
                bank = ps[:, B_CONV + s % 2, :].rearrange("p (w c) -> p w c", w=2)
                pieces = []
                for d in (0, -1, 1):
                    if 0 <= w + d and w + d + 2 <= W and (w + d) % RING != RING - 1:
                        pieces.append((0, 2, (w + d) % RING))
                    else:
                        pieces += [(i, 1, (w + d + i) % RING) for i in range(2) if 0 <= w + d + i < W]
                wait(pe, x1_done, 4 * c + s - 1)
                if s in (0, 1, 3):
                    pe.wait_ge(lo_ready, 2 * c + (1 if s == 0 else 2 if s == 1 or jc == CHUNKS - 1 else 3))
                n = 0
                for src in (nhi, nlo):
                    for i, k, at in pieces:
                        n += 1
                        ins = pe.matmul(bank[:, i:i + k, :], band[:, :], src[:, at:at + k, :],
                                        start=n == 1, stop=n == 2 * len(pieces))
                ins.then_inc(conv_done, 1)

            def step(t, j, pair):
                conv = chunk_at(t, j, pair, 2)
                ffn = chunk_at(t, j, pair, 4)
                back = chunk_at(t, j, pair, 5)
                if ffn:
                    c = ffn[0]
                    pe.wait_ge(feat_ready, c + 1)
                    wait(pe, ft_copied, c)
                    for b in range(CW):
                        at = (b % 2) * 4 * P + b // 2 * P
                        ins = pe.transpose(ftp[:, at:at + P], feat[:, j % 2, b, :], identb[:, :])
                    ins.then_inc(ft_done, 1)
                for s in range(GROUPS):
                    if conv:
                        convolve(conv, s)
                    tau = 4 * (t - 4) + s - 1
                    if not known(tau) or 0 <= tau < 4 * NCHUNK:
                        half = (s - 1) % 4 // 2
                        cur = (j if s > 0 else j - 1) % 2
                        pe.wait_ge(h1m_ready, tau + 1)
                        wait(pe, h2_ready, tau)
                        pe.matmul(ps[:, B_L2, :], w1[:, 4, :], featT[:, cur, half, :], start=True, stop=False)
                        pe.matmul(ps[:, B_L2, :], w2m[:, :], h1m[:, (s - 1) % 2, :], start=False, stop=False)
                        pe.wait_ge(h1lo_ready, tau + 1)
                        pe.matmul(ps[:, B_L2, :], w2r[:, :], h1r[:, (s - 1) % 2, :], start=False,
                                  stop=True).then_inc(l2_done, 1)
                    tau = 4 * (t - 4) + s - 2
                    if not known(tau) or 0 <= tau < 4 * NCHUNK:
                        tile = (s - 2) % 4
                        if tile == 0:
                            wait(pe, y_copied, t - 4)
                        pe.wait_ge(h2_ready, tau + 1)
                        pe.matmul(ps[32 * tile:32 * tile + 32, B_Y, :], w3[:, :], h2[:, s % 2, :],
                                  start=True, stop=True).then_inc(l3_done, 1)
                    if ffn:
                        c = ffn[0]
                        tau = 4 * c + s
                        if s == 0:
                            pe.wait_ge(ft_copied, c + 1)
                        rhs = featT[:, j % 2, s // 2, :]
                        wait(pe, h1m_ready, tau)
                        pe.matmul(ps[:, B_L1M, :], w1[:, s % 2, :], rhs, start=True, stop=True).then_inc(l1m_done, 1)
                        wait(pe, h1lo_ready, tau)
                        pe.matmul(ps[:, B_L1R, :], w1[:, 2 + s % 2, :], rhs, start=True,
                                  stop=True).then_inc(l1r_done, 1)
                    if s == 3 and back:
                        c = back[0]
                        pe.wait_ge(y_copied, c + 1)
                        wait(pe, y_read, c)
                        for q in range(4):
                            ins = pe.transpose(ps[:, B_YT, q * P:(q + 1) * P], ysb[:, q * P:(q + 1) * P], ident)
                        ins.then_inc(yt_done, 1)

            run_steps(pe, step)


W_DMAS = 8 + 12 + 8
SETUP_V = 10
AGG_STEPS, LN_STEPS = 4, 8
HOT_STEPS = 8
DEC_STEPS = 7


def constants():
    import numpy as np

    k = np.zeros((P, K_N), np.float32)
    k[:, K_ID:K_ID + P] = np.eye(P)
    rows = np.arange(P)
    near = (np.abs(rows[:, None] - rows[None, :]) <= 1) & (rows[:, None] // H == rows[None, :] // H)
    k[:, K_BAND:K_BAND + P] = near / SCALE
    k[:, K_RANK:K_RANK + 3 * NIB] = np.tile(NIB - np.arange(NIB), 3)
    k[:, K_IOTA:K_IOTA + NIB] = np.arange(NIB) + 1
    k[:, K_ISA] = rows < D
    k[:, K_ISS] = rows >= D
    k[:, K_T80] = rows == D
    k[:, K_T81] = rows == D + 1
    k[:, K_EPS:K_EPS + CW] = 1e-6
    k[:, K_EPS + CW:] = 1e-5
    return k


def kernel(x, L0_ffn_Wa, L0_ffn_ba, L0_ffn_Ws, L0_ffn_bs):
    import numpy as np
    import concourse.bacc as bacc
    from concourse.bass_utils import run_bass_kernel_spmd

    nc = bacc.Bacc("TRN2", target_bir_lowering=False, num_devices=1)
    arrays = {"x": x, "wa": L0_ffn_Wa, "ba": L0_ffn_ba, "ws": L0_ffn_Ws, "bs": L0_ffn_bs, "cst": constants()}
    arrays = {k: np.ascontiguousarray(a) for k, a in arrays.items()}
    aps = [nc.dram_tensor(k, a.shape, mybir.dt.from_np(a.dtype), kind="ExternalInput").ap()
           for k, a in arrays.items()]
    out = nc.dram_tensor("out", (B, C, H, W), F32, kind="ExternalOutput").ap()
    build(nc, *aps, out)
    r = run_bass_kernel_spmd(nc, [arrays], core_ids=[0])
    return r.results[0]["out"]
```

```python
from contextlib import ExitStack

import concourse.bass as bass
from concourse import mybir

F32 = mybir.dt.float32
F32R = mybir.dt.float32r
F16 = mybir.dt.float16
BF16 = mybir.dt.bfloat16
ALU = mybir.AluOpType
ACT = mybir.ActivationFunctionType

B, C, H, W = 8, 256, 64, 64
P = 128
D = 80
IMGS = P // H
PAIRS = B // IMGS
CW = 8
CHUNKS = W // CW
NCHUNK = PAIRS * CHUNKS
HALF = CW // 2
RING = 16
GROUPS = CW // 2
QC = 4
LATE = 1
EARLY = [q for q in range(QC) if q != LATE]
FIRST_PARTS = (0, W // 4, W // 2)
LAST_PARTS = (0, W // 4, W // 2, 3 * W // 4, W)

ALU_LO, ALU_HI, AX_LO, OP_COL, OUT_LO, OUT_HI, CARRY = 16, 32, 48, 65, 64, 72, 80
NIB = 16
UC = OP_COL + 2
OP_ADD_F = 35
RESULT = 50
CARRY_F = D - 1
MAIN = P - D
REM = D - MAIN

NV = 11
V_LO, V_HI, V_ONE = 6, 8, 10
PARTS = 3
ROWS = 2 * PARTS * NV

SCALE = 2048.0
MAGIC = 1.5 * 2.0 ** 23

K_ID, K_BAND, K_RANK, K_IOTA, K_ISA, K_ISS, K_T80, K_T81, K_EPS = 0, 128, 256, 304, 320, 321, 322, 323, 324
K_N = K_EPS + 2 * CW

B_CONV, B_L1M, B_L1R, B_L2, B_FT, B_Y, B_YT = 0, 2, 3, 4, 5, 6, 7

LAST_STEP = NCHUNK + 6


class Chain:

    def __init__(self, eng, sem, per):
        self.eng, self.sem, self.per, self.n = eng, sem, per, 0

    def turn(self, i, n=0):
        self.base, self.n = i * self.per, n

    def count(self, ins):
        ins.then_inc(self.sem, 1)
        self.n += 1

    def wait(self):
        wait(self.eng, self.sem, self.base + self.n)

    def end(self):
        assert self.n == self.per, (self.n, self.per)


def known(i):
    return isinstance(i, int)


def wait(eng, sem, value):
    if not known(value) or value > 0:
        eng.wait_ge(sem, value)


def chunk_at(t, j, pair, lag):
    c = t - lag
    if known(c) and not 0 <= c < NCHUNK:
        return None
    behind = 1 if lag > j else 0
    return c, (j - lag) % CHUNKS, (pair + behind) % 2


def tile_at(t, j, s, lag):
    behind = (lag - s + GROUPS - 1) // GROUPS
    c = t - 4 - behind
    if known(c) and not 0 <= c < NCHUNK:
        return None
    s = (s - lag) % GROUPS
    return GROUPS * c + s, s, c, (j - 4 - behind) % CHUNKS


def run_steps(eng, step):
    for t in range(CHUNKS):
        step(t, t, 0)
    with eng.Fori(1, PAIRS) as pair:
        for j in range(CHUNKS):
            with eng.register(f"pair_{eng.engine.name}_{j}") as copy:
                eng.reg_mov(copy, pair)
                here = eng.snap(copy, min_val=1, max_val=PAIRS - 1)
                step(here * CHUNKS + j, j, here)
    for t in range(NCHUNK, LAST_STEP):
        step(t, t % CHUNKS, t // CHUNKS)


def build(nc, x_d, wa_d, ba_d, ws_d, bs_d, cst_d, out_d):
    with ExitStack() as ctx:
        def sb(name, shape, dt):
            return ctx.enter_context(nc.sbuf_tensor(name, shape, dt))

        def sem(name):
            return ctx.enter_context(nc.semaphore(name))

        xbuf = sb("xbuf", [P, 2 * C * W], F32)
        n32 = sb("n32", [P, 2, HALF, C], F32)
        nhi = sb("nhi", [P, RING, C], F16)
        nlo = sb("nlo", [P, RING, C], F16)
        cst = sb("consts", [P, K_N], F32)
        band = sb("band", [P, P], F16)
        identb = sb("identb", [P, P], BF16)
        stat = sb("stat", [P, 2 * CW, 6], F32)
        s_sum = sb("s_sum", [P, 2 * CW], F32)
        s_dif = sb("s_dif", [P, 2 * CW], F32)
        s_m2 = sb("s_m2", [P, 2 * CW], F32)
        s_dd = sb("s_dd", [P, 2 * CW], F32)
        s_var = sb("s_var", [P, 2, 2 * CW], F32)
        s_sqrt = sb("s_sqrt", [P, 2, 2 * CW], F32)
        s_r0 = sb("s_r0", [P, 2 * CW], F32)
        s_nt = sb("s_nt", [P, 2 * CW], F32)
        s_nu = sb("s_nu", [P, 2 * CW], F32)
        mean = sb("mean", [P, 4, 2 * CW], F32)
        rstd = sb("rstd", [P, 4, 2 * CW], F32)
        rn = sb("rn", [P, 4, CW], F32)
        gain = sb("gain", [P, 4, CW], F32)
        shift = sb("shift", [P, 4, CW], F32)
        ut = sb("ut", [P, CW, UC], F32)
        u = sb("u", [P, CW, UC], F32)
        g = sb("g", [P, CW, 3 * NIB], F32)
        gw = sb("gw", [P, CW, 3, NIB], F32)
        mx1 = sb("mx1", [P, CW, 3], F32)
        nfree = sb("nfree", [P, CW, 3], F32)
        nhit = sb("nhit", [P, CW, 3], F32)
        marks = sb("marks", [P, CW, 3], F32)
        noadd = sb("noadd", [P, CW], F32)
        subraw = sb("subraw", [P, CW], F32)
        xres = sb("xres", [P, CW, 2], F32)
        msk = sb("msk", [P, 4, 3, CW], F32)
        val = sb("val", [P, CW, NV], BF16)
        feat = sb("feat", [P, 2, CW, P], BF16)
        featT = sb("featT", [P, 2, 2, 4 * P], BF16)
        h1m = sb("h1m", [P, 2, 512], F32)
        h1r = sb("h1r", [P, 2, 512], F32R)
        h2 = sb("h2", [P, 2 * GROUPS, 512], F32)
        ysb = sb("ysb", [P, 512], F32)
        ya = sb("ya", [P, CW, 2, 2], F32)
        ys = sb("ys", [P, CW, 2, 2], F32)
        yy = sb("yy", [P, CW, 2, 2], F32)
        yc = sb("yc", [P, CW, 2], F32)
        yr = sb("yr", [P, CW, 2], F32)
        yrr = sb("yrr", [P, CW, 2], F32)
        ycar = sb("ycar", [P, CW], F32)
        ycar2 = sb("ycar2", [P, CW], F32)
        hot = sb("hot", [P, CW, 2, NIB], F32)
        raw = h2[:, :, :].rearrange("p b n -> p (b n)")
        nat = raw[:, 0:2 * D].rearrange("p (k d) -> p k d", k=2)
        nat2, nat2r, nat3 = (raw[:, (2 + k) * P:(3 + k) * P] for k in range(3))
        tl = raw[:, 5 * P:5 * P + 5 * P // 2].bitcast(BF16) \
            .rearrange("p (k n) -> p k n", k=5)
        natb = sb("natb", [P, 2], F32)
        b2 = sb("b2", [P, 2], F32)
        base, res, res2 = (raw[:, k * P:k * P + 3 * NV].rearrange("p (k v) -> p k v", k=3) for k in (8, 9, 10))
        part = sb("part", [P, 3, PARTS, NV], BF16)
        w1 = sb("w1", [P, 5, P], BF16)
        w2m = sb("w2m", [P, P], F32)
        w2r = sb("w2r", [P, P], F32R)
        w3 = sb("w3", [P, 32], F32)

        ps = ctx.enter_context(nc.psum_tensor("ps", [P, 8, 512], F32))
        ftp = ps[:, B_FT, :].bitcast(BF16)
        ytv = ps[:, B_YT, :].rearrange("p (b m o) -> p b m o", b=CW, m=2)

        cst_loaded = sem("cst_loaded")
        w_loaded = sem("w_loaded")
        zeroed = sem("zeroed")
        band_ready = sem("band_ready")
        setup_v = sem("setup_v")
        setup_pe = sem("setup_pe")
        first_loaded = [sem(f"first_loaded{i}") for i in range(len(FIRST_PARTS) - 1)]
        x_loaded = sem("x_loaded")
        stored = [sem(f"stored{q}") for q in range(QC)]
        last_stored = sem("last_stored")
        ln = sem("ln")
        var_ready = sem("var_ready")
        sqrt_ready = sem("sqrt_ready")
        fin_ready = sem("fin_ready")
        n_ready = sem("n_ready")
        hi_ready = sem("hi_ready")
        lo_ready = sem("lo_ready")
        conv_done = sem("conv_done")
        x1_done = sem("x1_done")
        u_read = sem("u_read")
        dec = sem("dec")
        rank_ready = sem("rank_ready")
        top_ready = sem("top_ready")
        feat_ready = sem("feat_ready")
        ft_done = sem("ft_done")
        ft_copied = sem("ft_copied")
        l1m_done = sem("l1m_done")
        l1r_done = sem("l1r_done")
        h1m_ready = sem("h1m_ready")
        h1hi_ready = sem("h1hi_ready")
        h1lo_ready = sem("h1lo_ready")
        l2_done = sem("l2_done")
        h2_ready = sem("h2_ready")
        l3_done = sem("l3_done")
        y_copied = sem("y_copied")
        yt_done = sem("yt_done")
        y_read = sem("y_read")
        out_ready = sem("out_ready")
        hotc = sem("hotc")

        def xview(parity):
            lo = parity * (C * W)
            return xbuf[:, bass.ds(lo, C * W)].rearrange("p (c w) -> p w c", w=W)

        def over(ap, shape):
            return ap.broadcast_to(shape)

        block = ctx.enter_context(nc.Block())

        @block.sync
        def _(sp):
            def tile_part(parity, img, q):
                n = C // QC * W
                return xbuf[img * H:(img + 1) * H, bass.ds(parity * (C * W) + q * n, n)] \
                    .rearrange("p (c w) -> p c w", w=W)

            def dram_part(ap, pair, img, q):
                cs = slice(q * (C // QC), (q + 1) * (C // QC))
                return ap[bass.ds(pair * IMGS + img, 1), cs].rearrange("b c h w -> (b h) c w")

            def load(pair, parity, q):
                for img in range(IMGS):
                    sp.dma_start(tile_part(parity, img, q), dram_part(x_d, pair, img, q)).then_inc(x_loaded, 16)

            def store(pair, q):
                for img in range(IMGS):
                    sp.dma_start(dram_part(out_d, pair, img, q), tile_part(pair % 2, img, q)) \
                        .then_inc(stored[q], 16)

            def columns(parity, img, c0, c1, w0, w1):
                return xbuf[img * H:(img + 1) * H, bass.ds(parity * (C * W) + c0 * W, (c1 - c0) * W)] \
                    .rearrange("p (c w) -> p c w", w=W)[:, :, w0:w1]

            def image(ap, b, c0, c1, w0, w1):
                return ap[b:b + 1, c0:c1, :, w0:w1].rearrange("b c h w -> (b h) c w")

            def load_weights():
                sp.wait_ge(zeroed, 1)
                loads = [
                    (nat[0:D, 0, :], wa_d[0]), (nat[D:P, 0, :], ws_d[0, 0:MAIN]),
                    (nat2[0:D, 0:D], wa_d[1]), (nat2[0:D, D:P], ws_d[1, :, 0:MAIN]),
                    (natb[0:D, 0:1], ba_d[0].unsqueeze(1)), (natb[D:P, 0:1], bs_d[0, 0:MAIN].unsqueeze(1)),
                    (b2[0:D, 0:1], ba_d[1].unsqueeze(1)), (b2[0:D, 1:2], bs_d[1].unsqueeze(1)),
                ]
                for q in range(4):
                    rows = slice(REM * q, REM * (q + 1))
                    loads += [(nat[rows, 1, :], ws_d[0, MAIN:D]), (nat2r[0:D, rows], ws_d[1, :, MAIN:D]),
                              (natb[rows, 1:2], bs_d[0, MAIN:D].unsqueeze(1))]
                for i, (w_d, b_d, f) in enumerate(((wa_d, ba_d, RESULT), (wa_d, ba_d, CARRY_F),
                                                   (ws_d, bs_d, RESULT), (ws_d, bs_d, CARRY_F))):
                    at = D + i // 2
                    loads += [(nat3[i:i + 1, 0:D], w_d[2, f:f + 1]), (nat3[i:i + 1, at:at + 1], b_d[2:3, f:f + 1])]
                assert len(loads) == W_DMAS
                for dst, src in loads:
                    sp.dma_start(dst, src).then_inc(w_loaded, 16)

            per_pair = 16 * IMGS * QC
            sp.dma_start(cst[:, :], cst_d).then_inc(cst_loaded, 16)
            for i, (w0, w1) in enumerate(zip(FIRST_PARTS, FIRST_PARTS[1:])):
                for img in range(IMGS):
                    sp.dma_start(columns(0, img, 0, C, w0, w1), image(x_d, img, 0, C, w0, w1)) \
                        .then_inc(first_loaded[i], 16)
                if i == 0:
                    load_weights()
            for q in range(QC):
                for img in range(IMGS):
                    part = q * C // QC, (q + 1) * C // QC, FIRST_PARTS[-1], W
                    sp.dma_start(columns(0, img, *part), image(x_d, img, *part)).then_inc(x_loaded, 16)
            sp.wait_ge(x_loaded, per_pair)
            for q in range(QC):
                load(1, 1, q)

            def leave(pair):
                sp.wait_ge(out_ready, (pair + 1) * CHUNKS)
                for q in EARLY:
                    store(pair, q)

            def leave_late(pair):
                sp.wait_ge(hotc, (pair + 1) * (CHUNKS * HOT_STEPS))
                store(pair, LATE)

            def enter(pair, q):
                sp.wait_ge(stored[q], 16 * IMGS * (pair + 1))
                load(pair + 2, pair % 2, q)

            with sp.Fori(0, PAIRS - 2) as pair:
                sp.wait_ge(x_loaded, per_pair * (pair + 2))
                leave(pair)
                for q in EARLY:
                    enter(pair, q)
                leave_late(pair)
                enter(pair, LATE)
            leave(PAIRS - 2)
            leave_late(PAIRS - 2)
            pair, left = PAIRS - 1, 0
            late = (LATE * C // QC, (LATE + 1) * C // QC)
            for w0, w1 in zip(LAST_PARTS, LAST_PARTS[1:]):
                chunks = pair * CHUNKS + w1 // CW
                for c0, c1 in ((0, late[0]), (late[1], C), late):
                    if (c0, c1) != late:
                        sp.wait_ge(out_ready, chunks)
                    else:
                        sp.wait_ge(hotc, chunks * HOT_STEPS)
                    for img in range(IMGS):
                        b = pair * IMGS + img
                        sp.dma_start(image(out_d, b, c0, c1, w0, w1),
                                     columns(pair % 2, img, c0, c1, w0, w1)).then_inc(last_stored, 16)
                        left += 16
            for q in range(QC):
                sp.wait_ge(stored[q], 16 * IMGS * (PAIRS - 1))
            sp.wait_ge(last_stored, left)

        @block.vector
        def _(v):
            v.memset(nat2[:, :], 0.0)
            v.memset(nat2r[:, :], 0.0)
            v.memset(nat3[:, :], 0.0)
            v.memset(b2[:, :], 0.0)
            v.memset(base[:, :, :], 0.0).then_inc(zeroed, 1)
            v.memset(tl[:, :, :], 0.0)
            v.memset(feat[:, :, :, :], 0.0)
            v.memset(stat[:, :, :], 0.0)
            v.memset(val[:, :, V_ONE:V_ONE + 1], 1.0).then_inc(zeroed, 1)
            n_setup = [0]

            def done(ins):
                n_setup[0] += 1
                ins.then_inc(setup_v, 1)
                v.wait_ge(setup_v, n_setup[0])

            v.wait_ge(zeroed, 2)
            v.wait_ge(cst_loaded, 16)
            v.tensor_copy(identb[:, :], cst[:, K_ID:K_ID + P])
            v.tensor_copy(band[:, :], cst[:, K_BAND:K_BAND + P]).then_inc(band_ready, 1)

            def setup_parts():
                v.wait_ge(w_loaded, W_DMAS * 16)
                for k in range(2):
                    for j in range(PARTS):
                        v.tensor_copy(base[:, k, 2 * j:2 * j + 2], nat[:, k, OP_ADD_F:OP_ADD_F + 2])
                    for at in (V_LO, V_HI):
                        v.tensor_copy(base[:, k, at:at + 2], nat[:, k, 0:2])
                    v.tensor_copy(base[:, k, V_ONE:V_ONE + 1], natb[:, k:k + 1])
                done(v.tensor_copy(base[:, 2, 0:2], b2[:, :]))
                done(v.tensor_copy(part[:, :, 0, :], base[:, :, :]))
                done(v.tensor_tensor(res[:, :, :], base[:, :, :], part[:, :, 0, :], ALU.subtract))
                done(v.tensor_copy(part[:, :, 1, :], res[:, :, :]))
                done(v.tensor_tensor(res2[:, :, :], res[:, :, :], part[:, :, 1, :], ALU.subtract))
                done(v.tensor_copy(part[:, :, 2, :], res2[:, :, :]))
                flat = part[:, :, :, :].rearrange("p k j v -> p k (j v)")
                half = PARTS * NV
                for pos in range(2):
                    v.tensor_scalar(tl[:, pos, 0:half], flat[:, 0, :], cst[:, K_ISA:K_ISA + 1], None, ALU.mult)
                    v.tensor_scalar(tl[:, pos, half:2 * half], flat[:, 0, :], cst[:, K_ISS:K_ISS + 1], None, ALU.mult)
                    v.tensor_copy(tl[:, 2 + pos, half:2 * half], flat[:, 1, :])
                for m in range(2):
                    for j in range(PARTS):
                        at = (m * PARTS + j) * NV + V_ONE
                        if j == 0:
                            one = K_T80 if m == 0 else K_T81
                            ins = v.tensor_tensor(tl[:, 4, at:at + 1], part[:, 2, j, m:m + 1], cst[:, one:one + 1],
                                                  ALU.add)
                        else:
                            ins = v.tensor_copy(tl[:, 4, at:at + 1], part[:, 2, j, m:m + 1])
                done(ins)
                for k in range(4):
                    at = V_HI if k % 2 == 0 else V_LO
                    rows = tl[:, k, 0:ROWS].rearrange("p (r v) -> p r v", v=NV)
                    ins = v.memset(rows[:, :, at:at + 2], 0.0)
                done(ins)

            def setup_weights():
                v.wait_ge(setup_pe, 1)
                v.tensor_copy(w1[:, :, :], ftp[:, 0:5 * P].rearrange("p (k n) -> p k n", k=5))
                wt = ps[:, B_YT, :].rearrange("p (k n) -> p k n", k=4)
                v.tensor_copy(w2m[:, :], wt[:, 0, :])
                v.tensor_copy(w3[:, :], wt[:, 2, 0:32])
                done(v.tensor_copy(w2r[:, :], wt[:, 1, :]))
                for q in (1, 3):
                    rows = slice(32 * q, 32 * q + 32)
                    ins = v.tensor_tensor(w2r[rows, :], wt[rows, 1, :], w2r[rows, :], ALU.subtract)
                done(ins)
                assert n_setup[0] == SETUP_V

            lnc = Chain(v, ln, LN_STEPS)
            hc = Chain(v, hotc, HOT_STEPS)
            four = [P, CW, 2, 2]
            hot_shape = [P, CW, 2, NIB]

            def variance(i, t, j):
                lnc.wait()
                if i == 0:
                    wait(v, out_ready, t - 5)
                    v.tensor_tensor(s_sum[:, :], stat[:, :, 1], stat[:, :, 4], ALU.add)
                    v.tensor_tensor(s_dif[:, :], stat[:, :, 1], stat[:, :, 4], ALU.subtract)
                    lnc.count(v.tensor_tensor(s_m2[:, :], stat[:, :, 2], stat[:, :, 5], ALU.add))
                elif i == 1:
                    v.tensor_scalar(mean[:, j % 4, :], s_sum[:, :], 0.5, None, ALU.mult)
                    v.scalar_tensor_tensor(s_dd[:, :], s_dif[:, :], 0.25, s_dif[:, :], ALU.mult, ALU.mult)
                    lnc.count(v.scalar_tensor_tensor(s_m2[:, :], s_m2[:, :], 1.0 / C,
                                                     cst[:, K_EPS:K_EPS + 2 * CW], ALU.mult, ALU.add))
                else:
                    lnc.count(v.tensor_tensor(s_var[:, j % 2, :], s_m2[:, :], s_dd[:, :], ALU.add))

            def sigma(i, t, j):
                k, b = (j - 1) % 4, (j - 1) % 2
                if i == 0:
                    lnc.turn(t - 1, AGG_STEPS)
                    v.wait_ge(sqrt_ready, t)
                    lnc.count(v.reciprocal(s_r0[:, :], s_sqrt[:, b, :]))
                    return
                lnc.wait()
                if i == 1:
                    lnc.count(v.scalar_tensor_tensor(s_nt[:, :], s_r0[:, :], -0.5, s_r0[:, :], ALU.mult, ALU.mult))
                elif i == 2:
                    lnc.count(v.tensor_tensor(s_nu[:, :], s_nt[:, :], s_var[:, b, :], ALU.mult))
                elif i == 3:
                    lnc.count(v.scalar_tensor_tensor(rstd[:, k, :], s_nu[:, :], 1.5, s_r0[:, :], ALU.add, ALU.mult))
                    lnc.end()
                else:
                    v.tensor_scalar(rn[:, k, :], rstd[:, k, 0:CW], SCALE / 9.0, None, ALU.mult)
                    v.tensor_scalar(gain[:, k, :], rstd[:, k, CW:], 1.0, None, ALU.add)
                    v.scalar_tensor_tensor(shift[:, k, :], mean[:, k, CW:], -1.0, rstd[:, k, CW:],
                                           ALU.mult, ALU.mult).then_inc(fin_ready, 1)

            def result(i, last, k):
                c, jc, par = last
                cols = xview(par)[:, jc * CW:(jc + 1) * CW, :]
                add, sub, act = (msk[:, k, n, :] for n in range(3))
                if i == 0:
                    hc.turn(c)
                    hc.wait()
                    v.wait_ge(feat_ready, c + 1)
                    v.wait_ge(yt_done, c + 1)
                    v.tensor_tensor(ya[:, :, :, :], ytv[:, :, :, 0:2],
                                    over(add.unsqueeze(2).unsqueeze(3), four), ALU.mult)
                    v.tensor_tensor(ys[:, :, :, :], ytv[:, :, :, 2:4],
                                    over(sub.unsqueeze(2).unsqueeze(3), four), ALU.mult).then_inc(y_read, 1)
                    return
                if i == 1:
                    v.wait_ge(y_read, c + 1)
                    hc.count(v.tensor_tensor(yy[:, :, :, :], ya[:, :, :, :], ys[:, :, :, :], ALU.add))
                    return
                hc.wait()
                if i == 2:
                    v.tensor_scalar(ycar[:, :], yy[:, :, 1, 1], 0.5, None, ALU.is_gt)
                    hc.count(v.tensor_scalar(yc[:, :, :], yy[:, :, :, 0], 0.0, float(NIB - 1), ALU.max, ALU.min))
                elif i == 3:
                    v.tensor_tensor(ycar2[:, :], ycar[:, :], act, ALU.mult)
                    hc.count(v.tensor_scalar(yr[:, :, :], yc[:, :, :], MAGIC, MAGIC, ALU.add, ALU.subtract))
                elif i == 4:
                    hc.count(v.scalar_tensor_tensor(yrr[:, :, :], yr[:, :, :], 1.0,
                                                    over(act.unsqueeze(2), [P, CW, 2]), ALU.add, ALU.mult))
                elif i == 5:
                    hc.count(v.tensor_tensor(hot[:, :, :, :],
                                             over(cst[:, K_IOTA:K_IOTA + NIB].unsqueeze(1).unsqueeze(2), hot_shape),
                                             over(yrr[:, :, :].unsqueeze(3), hot_shape), ALU.is_equal))
                elif i in (6, 7):
                    at = OUT_LO if i == 6 else OUT_HI
                    v.wait_ge(out_ready, c + 1)
                    hc.count(v.scalar_tensor_tensor(cols[:, :, at:at + NIB], hot[:, :, i - 6, :], 2.0,
                                                    cols[:, :, at:at + NIB], ALU.mult, ALU.add))
                else:
                    hc.count(v.tensor_tensor(cols[:, :, CARRY], cols[:, :, CARRY], ycar2[:, :], ALU.add))
                    hc.end()

            def step(t, j, pair):
                first = chunk_at(t, j, pair, 0)
                norm = chunk_at(t, j, pair, 1)
                conv = chunk_at(t, j, pair, 2)
                tok = chunk_at(t, j, pair, 3)
                last = chunk_at(t, j, pair, 6)
                ends = not known(t) or t <= NCHUNK + 1
                begins = not known(t) or 1 <= t <= NCHUNK + 2

                def finish(i):
                    if begins:
                        sigma(i, t, j)

                def put(i):
                    if last:
                        result(i, last, (j - 6) % 4)

                def normalise(w):
                    if norm:
                        c, jc, par = norm
                        if w == 0:
                            v.wait_ge(fin_ready, t)
                        if w % HALF == 0:
                            wait(v, lo_ready, 2 * c + w // HALF - 1)
                        k = (j - 1) % 4
                        ins = v.tensor_scalar(n32[:, w // HALF, w % HALF, :], xview(par)[:, jc * CW + w, :],
                                              mean[:, k, w:w + 1], rn[:, k, w:w + 1], ALU.subtract, ALU.mult)
                        if w % HALF == HALF - 1:
                            ins.then_inc(n_ready, 1)

                def x_statistics(i):
                    if first:
                        c, jc, par = first
                        return v.bn_stats(stat[:, i, :], xview(par)[:, jc * CW + i, :])

                def x1_statistics(i):
                    if conv:
                        c, jc, par = conv
                        return v.bn_stats(stat[:, CW + i, :], xview(par)[:, jc * CW + i, :])

                def add_convolution(s):
                    if conv:
                        c, jc, par = conv
                        w = jc * CW + 2 * s
                        pair_cols = xview(par)[:, w:w + 2, :]
                        v.wait_ge(conv_done, 4 * c + s + 1)
                        v.tensor_tensor(pair_cols, ps[:, B_CONV + s % 2, :].rearrange("p (w c) -> p w c", w=2),
                                        pair_cols, ALU.add).then_inc(x1_done, 1)

                def low_parts(s):
                    if conv and s > 0:
                        v.wait_ge(x1_done, 4 * conv[0] + s)
                    tile = tile_at(t, j, s, 2)
                    if tile:
                        tau, i = tile[:2]
                        low = h1r[64:, i % 2, :]
                        v.wait_ge(h1hi_ready, tau + 1)
                        v.scalar_tensor_tensor(low, ps[64:, B_L1R, :], 0.0, low,
                                               ALU.max, ALU.subtract).then_inc(h1lo_ready, 1)

                if known(t) and t == 3:
                    setup_parts()
                if known(t) and t == 4:
                    setup_weights()
                low_parts(0)
                finish(0)
                if known(t) and t * CW in FIRST_PARTS[:-1]:
                    v.wait_ge(first_loaded[FIRST_PARTS.index(t * CW)], 16 * IMGS)
                elif first and (t * CW == FIRST_PARTS[-1] if known(t) else j == 0):
                    v.wait_ge(x_loaded, (pair + 1) * 16 * IMGS * QC)
                add_convolution(0)
                finish(1)
                x_statistics(0)
                finish(2)
                finish(3)
                x_statistics(1)
                finish(4)
                for w in range(HALF):
                    normalise(w)

                low_parts(1)
                x1_statistics(0)
                x1_statistics(1)
                add_convolution(1)
                x_statistics(2)
                x_statistics(3)
                for w in range(HALF, CW):
                    put(w - HALF)
                    normalise(w)

                low_parts(2)
                x1_statistics(2)
                add_convolution(2)
                x_statistics(4)
                x1_statistics(3)
                put(4)
                x_statistics(5)

                if tok:
                    v.wait_ge(rank_ready, tok[0] + 1)
                    v.tensor_reduce(mx1[:, :, :], gw[:, :, :, :], mybir.AxisListType.X,
                                    ALU.max).then_inc(top_ready, 1)
                low_parts(3)
                x1_statistics(4)
                add_convolution(3)
                x_statistics(6)
                x1_statistics(5)
                counted = x_statistics(7)
                if conv:
                    v.wait_ge(x1_done, 4 * conv[0] + 4)
                put(5)
                x1_statistics(6)
                counted = x1_statistics(7) or counted
                if ends:
                    lnc.turn(t)
                    lnc.count(counted)
                for i in range(3):
                    if ends:
                        variance(i, t, j)
                    put(6 + i)

            run_steps(v, step)

        @block.gpsimd
        def _(pool):
            dc = Chain(pool, dec, DEC_STEPS)

            def step(t, j, pair):
                norm = chunk_at(t, j, pair, 1)
                tok = chunk_at(t, j, pair, 3)
                k4 = (j - 3) % 4

                def low_parts(h):
                    c, jc, par = norm
                    at = (jc * CW + h * HALF) % RING
                    pool.wait_ge(hi_ready, 2 * c + h + 1)
                    pool.tensor_tensor(nlo[:, at:at + HALF, :], n32[:, h, :, :], nhi[:, at:at + HALF, :],
                                       ALU.subtract).then_inc(lo_ready, 1)

                if tok:
                    c, jc, par = tok
                    dc.turn(c)
                    dc.wait()
                    pool.wait_ge(fin_ready, t)
                    shape = [P, CW, UC]
                    dc.count(pool.tensor_tensor(ut[:, :, :], xview(par)[:, jc * CW:(jc + 1) * CW, 0:UC],
                                               over(mean[:, (j - 1) % 4, CW:].unsqueeze(2), shape), ALU.subtract))
                    dc.wait()
                    pool.tensor_tensor(u[:, :, :], ut[:, :, :],
                                       over(rstd[:, (j - 1) % 4, CW:].unsqueeze(2), shape),
                                       ALU.mult).then_inc(u_read, 1)
                    pool.wait_ge(u_read, c + 1)
                    wait(pool, hotc, (c - 3) * HOT_STEPS)
                if norm:
                    low_parts(0)
                if tok:
                    if known(c) and c == 0:
                        pool.wait_ge(zeroed, 2)
                        pool.wait_ge(cst_loaded, 16)
                    add, sub, act = (msk[:, k4, i, :] for i in range(3))
                    pool.tensor_scalar(g[:, :, :], u[:, :, ALU_LO:ALU_LO + 3 * NIB], 0.5, None, ALU.is_gt)
                    pool.tensor_scalar(marks[:, :, :], u[:, :, 0:3], 0.5, None, ALU.is_gt)
                    dc.count(pool.tensor_copy(val[:, :, 0:2], u[:, :, OP_COL:OP_COL + 2]))
                    dc.wait()
                    rank = cst[:, K_RANK:K_RANK + 3 * NIB]
                    pool.tensor_tensor(gw[:, :, :, :].rearrange("p b k n -> p b (k n)"), g[:, :, :],
                                       over(rank.unsqueeze(1), [P, CW, 3 * NIB]), ALU.mult).then_inc(rank_ready, 1)
                    pool.tensor_tensor(add, marks[:, :, 0], marks[:, :, 1], ALU.mult)
                    pool.tensor_tensor(subraw[:, :], marks[:, :, 0], marks[:, :, 2], ALU.mult)
                    pool.tensor_scalar(noadd[:, :], marks[:, :, 1], -1.0, 1.0, ALU.mult, ALU.add)
                    dc.count(pool.tensor_tensor(xres[:, :, :], u[:, :, OP_COL:OP_COL + 2], val[:, :, 0:2],
                                               ALU.subtract))
                    dc.wait()
                    pool.tensor_tensor(sub, subraw[:, :], noadd[:, :], ALU.mult)
                    dc.count(pool.tensor_copy(val[:, :, 2:4], xres[:, :, :]))
                    dc.wait()
                    pool.tensor_tensor(act, add, sub, ALU.add)
                    dc.count(pool.tensor_tensor(val[:, :, 4:6], xres[:, :, :], val[:, :, 2:4], ALU.subtract))
                if norm:
                    low_parts(1)
                if tok:
                    c = tok[0]
                    pool.wait_ge(top_ready, c + 1)
                    pool.tensor_tensor(nfree[:, :, :], over(rank[:, 0:1].unsqueeze(1), [P, CW, 3]), mx1[:, :, :],
                                       ALU.subtract)
                    dc.count(pool.tensor_scalar(nhit[:, :, :], mx1[:, :, :], 0.5, None, ALU.is_gt))
                    dc.wait()
                    pool.tensor_tensor(val[:, :, V_LO:V_LO + 2], nfree[:, :, 0:3:2], nhit[:, :, 0:3:2], ALU.mult)
                    dc.count(pool.tensor_tensor(val[:, :, V_HI:V_HI + 2],
                                               over(nfree[:, :, 1:2], [P, CW, 2]),
                                               over(nhit[:, :, 1:2], [P, CW, 2]), ALU.mult))
                    dc.wait()
                    wait(pool, ft_done, c - 1)
                    half = PARTS * NV
                    shape = [P, CW, PARTS, NV]
                    for m, mask in enumerate((add, sub)):
                        ins = pool.tensor_tensor(
                            feat[:, (j + 1) % 2, :, m * half:(m + 1) * half].rearrange("p b (j v) -> p b j v", v=NV),
                            over(val[:, :, :].unsqueeze(2), shape), over(mask.unsqueeze(2).unsqueeze(3), shape),
                            ALU.mult)
                    ins.then_inc(feat_ready, 1)
                    dc.end()
                    pool.wait_ge(feat_ready, c + 1)

            run_steps(pool, step)

        @block.scalar
        def _(act):
            def step(t, j, pair):
                norm = chunk_at(t, j, pair, 1)
                tok = chunk_at(t, j, pair, 3)
                ffn = chunk_at(t, j, pair, 4)
                back = chunk_at(t, j, pair, 5)
                for s in range(GROUPS):
                    tile = tile_at(t, j, s, 1)
                    if tile:
                        tau = tile[0]
                        act.wait_ge(l1r_done, tau + 1)
                        wait(act, l2_done, tau - 1)
                        act.activation(h1r[:, tile[1] % 2, :], ps[:, B_L1R, :], ACT.Relu).then_inc(h1hi_ready, 1)
                        act.wait_ge(l1m_done, tau + 1)
                        act.activation(h1m[:, tile[1] % 2, :], ps[:, B_L1M, :], ACT.Relu).then_inc(h1m_ready, 1)
                    if s == 0 and ffn:
                        c, jc, par = ffn
                        act.wait_ge(ft_done, c + 1)
                        wait(act, l2_done, 4 * c - 4)
                        act.activation(featT[:, jc % 2, :, :].rearrange("p a n -> p (a n)"), ftp,
                                       ACT.Copy).then_inc(ft_copied, 1)
                    if norm and s < 2:
                        c, jc, par = norm
                        at = (jc * CW + s * HALF) % RING
                        act.wait_ge(n_ready, 2 * c + s + 1)
                        wait(act, conv_done, 2 * (2 * c + s) - 5)
                        act.activation(nhi[:, at:at + HALF, :], n32[:, s, :, :], ACT.Copy).then_inc(hi_ready, 1)
                    tile = tile_at(t, j, s, 2)
                    if tile:
                        tau, i, c, jc = tile
                        act.wait_ge(l2_done, tau + 1)
                        wait(act, l3_done, c - 1)
                        act.activation(h2[:, GROUPS * (jc % 2) + i, :], ps[:, B_L2, :],
                                       ACT.Relu).then_inc(h2_ready, 1)
                    if s == 3 and back:
                        c = back[0]
                        act.wait_ge(l3_done, c + 1)
                        wait(act, yt_done, c)
                        act.activation(ysb[:, :], ps[:, B_Y, :], ACT.Copy).then_inc(y_copied, 1)
                    if tok:
                        c, jc, par = tok
                        if s == 0:
                            act.wait_ge(u_read, c + 1)
                        k = (j - 1) % 4
                        for w in (2 * s, 2 * s + 1):
                            col = xview(par)[:, jc * CW + w, :]
                            ins = act.activation(col, col, ACT.Identity, bias=shift[:, k, w:w + 1],
                                                 scale=gain[:, k, w:w + 1])
                        if s == 3:
                            ins.then_inc(out_ready, 1)
                if not known(t) or t <= NCHUNK + 1:
                    act.wait_ge(ln, LN_STEPS * t + AGG_STEPS)
                    act.activation(s_sqrt[:, j % 2, :], s_var[:, j % 2, :], ACT.Sqrt).then_inc(sqrt_ready, 1)

            run_steps(act, step)

        @block.tensor
        def _(pe):
            pe.wait_ge(band_ready, 1)
            ident = cst[:, K_ID:K_ID + P]

            def setup_weights():
                pe.wait_ge(setup_v, SETUP_V - 2)
                for k in range(5):
                    pe.transpose(ftp[:, k * P:(k + 1) * P], tl[:, k, :], identb[:, :])
                for k, src in enumerate((nat2, nat2r, nat3)):
                    ins = pe.transpose(ps[:, B_YT, k * P:(k + 1) * P], src[:, :], ident)
                ins.then_inc(setup_pe, 1)

            def convolve(conv, s):
                c, jc, par = conv
                w = jc * CW + 2 * s
                bank = ps[:, B_CONV + s % 2, :].rearrange("p (w c) -> p w c", w=2)
                pieces = []
                for d in (0, -1, 1):
                    if 0 <= w + d and w + d + 2 <= W and (w + d) % RING != RING - 1:
                        pieces.append((0, 2, (w + d) % RING))
                    else:
                        pieces += [(i, 1, (w + d + i) % RING) for i in range(2) if 0 <= w + d + i < W]
                wait(pe, x1_done, 4 * c + s - 1)
                if s in (0, 1, 3):
                    pe.wait_ge(lo_ready, 2 * c + (1 if s == 0 else 2 if s == 1 or jc == CHUNKS - 1 else 3))
                n = 0
                for src in (nhi, nlo):
                    for i, k, at in pieces:
                        n += 1
                        ins = pe.matmul(bank[:, i:i + k, :], band[:, :], src[:, at:at + k, :],
                                        start=n == 1, stop=n == 2 * len(pieces))
                ins.then_inc(conv_done, 1)

            def step(t, j, pair):
                conv = chunk_at(t, j, pair, 2)
                ffn = chunk_at(t, j, pair, 4)
                back = chunk_at(t, j, pair, 5)
                last = chunk_at(t, j, pair, 6)
                if known(t) and t == 3:
                    setup_weights()
                if known(t) and t == 4:
                    pe.wait_ge(setup_v, SETUP_V)
                for s in range(GROUPS):
                    if conv:
                        convolve(conv, s)
                    if s == 0 and ffn:
                        c, jc, par = ffn
                        pe.wait_ge(feat_ready, c + 1)
                        wait(pe, ft_copied, c)
                        for b in range(CW):
                            at = (b % 2) * 4 * P + b // 2 * P
                            ins = pe.transpose(ftp[:, at:at + P], feat[:, jc % 2, b, :], identb[:, :])
                        ins.then_inc(ft_done, 1)
                    tile = tile_at(t, j, s, 1)
                    if tile:
                        tau, i, c, jc = tile
                        if i == 0:
                            pe.wait_ge(ft_copied, c + 1)
                        rhs = featT[:, jc % 2, i // 2, :]
                        wait(pe, h1lo_ready, tau)
                        pe.matmul(ps[:, B_L1R, :], w1[:, 2 + i % 2, :], rhs, start=True,
                                  stop=True).then_inc(l1r_done, 1)
                        wait(pe, h1m_ready, tau)
                        pe.matmul(ps[:, B_L1M, :], w1[:, i % 2, :], rhs, start=True, stop=True).then_inc(l1m_done, 1)
                    tile = tile_at(t, j, s, 2)
                    if tile:
                        tau, i, c, jc = tile
                        pe.wait_ge(h1m_ready, tau + 1)
                        wait(pe, h2_ready, tau)
                        pe.matmul(ps[:, B_L2, :], w1[:, 4, :], featT[:, jc % 2, i // 2, :], start=True, stop=False)
                        pe.matmul(ps[:, B_L2, :], w2m[:, :], h1m[:, i % 2, :], start=False, stop=False)
                        pe.wait_ge(h1lo_ready, tau + 1)
                        pe.matmul(ps[:, B_L2, :], w2r[:, :], h1r[:, i % 2, :], start=False,
                                  stop=True).then_inc(l2_done, 1)
                    if s == 2 and back:
                        c, jc, par = back
                        wait(pe, y_copied, c)
                        pe.wait_ge(h2_ready, 4 * c + 4)
                        for i in range(GROUPS):
                            ins = pe.matmul(ps[32 * i:32 * i + 32, B_Y, :], w3[:, :],
                                            h2[:, GROUPS * (jc % 2) + i, :], start=True, stop=True)
                        ins.then_inc(l3_done, 1)
                    if s == 0 and last:
                        c = last[0]
                        pe.wait_ge(y_copied, c + 1)
                        wait(pe, y_read, c)
                        for q in range(4):
                            ins = pe.transpose(ps[:, B_YT, q * P:(q + 1) * P], ysb[:, q * P:(q + 1) * P], ident)
                        ins.then_inc(yt_done, 1)

            run_steps(pe, step)


W_DMAS = 8 + 12 + 8
SETUP_V = 10
AGG_STEPS, LN_STEPS = 4, 8
HOT_STEPS = 8
DEC_STEPS = 7


def constants():
    import numpy as np

    k = np.zeros((P, K_N), np.float32)
    k[:, K_ID:K_ID + P] = np.eye(P)
    rows = np.arange(P)
    near = (np.abs(rows[:, None] - rows[None, :]) <= 1) & (rows[:, None] // H == rows[None, :] // H)
    k[:, K_BAND:K_BAND + P] = near / SCALE
    k[:, K_RANK:K_RANK + 3 * NIB] = np.tile(NIB - np.arange(NIB), 3)
    k[:, K_IOTA:K_IOTA + NIB] = np.arange(NIB) + 1
    k[:, K_ISA] = rows < D
    k[:, K_ISS] = rows >= D
    k[:, K_T80] = rows == D
    k[:, K_T81] = rows == D + 1
    k[:, K_EPS:K_EPS + CW] = 1e-6
    k[:, K_EPS + CW:] = 1e-5
    return k


def kernel(x, L0_ffn_Wa, L0_ffn_ba, L0_ffn_Ws, L0_ffn_bs):
    import numpy as np
    import concourse.bacc as bacc
    from concourse.bass_utils import run_bass_kernel_spmd

    nc = bacc.Bacc("TRN2", target_bir_lowering=False, num_devices=1)
    arrays = {"x": x, "wa": L0_ffn_Wa, "ba": L0_ffn_ba, "ws": L0_ffn_Ws, "bs": L0_ffn_bs, "cst": constants()}
    arrays = {k: np.ascontiguousarray(a) for k, a in arrays.items()}
    aps = [nc.dram_tensor(k, a.shape, mybir.dt.from_np(a.dtype), kind="ExternalInput").ap()
           for k, a in arrays.items()]
    out = nc.dram_tensor("out", (B, C, H, W), F32, kind="ExternalOutput").ap()
    build(nc, *aps, out)
    r = run_bass_kernel_spmd(nc, [arrays], core_ids=[0])
    return r.results[0]["out"]
```

```python
from contextlib import ExitStack

import concourse.bass as bass
from concourse import mybir

F32 = mybir.dt.float32
F32R = mybir.dt.float32r
F16 = mybir.dt.float16
BF16 = mybir.dt.bfloat16
ALU = mybir.AluOpType
ACT = mybir.ActivationFunctionType

B, C, H, W = 8, 256, 64, 64
P = 128
D = 80
IMGS = P // H
PAIRS = B // IMGS
CW = 8
CHUNKS = W // CW
NCHUNK = PAIRS * CHUNKS
HALF = CW // 2
RING = 16
GROUPS = CW // 2
HALVES = 2
HALF_W = W // HALVES
EARLY = ((0, C // 4), (C // 2, C))
LATE = (C // 4, C // 2)
RANGES = EARLY + (LATE,)
FIRST_PART = W // 4
LAST_PARTS = (0, W // 4, W // 2, 3 * W // 4, W)

ALU_LO, ALU_HI, AX_LO, OP_COL, OUT_LO, OUT_HI, CARRY = 16, 32, 48, 65, 64, 72, 80
NIB = 16
UC = OP_COL + 2
OP_ADD_F = 35
RESULT = 50
CARRY_F = D - 1
MAIN = P - D
REM = D - MAIN

NV = 11
V_LO, V_HI, V_ONE = 6, 8, 10
PARTS = 3
ROWS = 2 * PARTS * NV

SCALE = 2048.0
MAGIC = 1.5 * 2.0 ** 23

K_ID, K_BAND, K_RANK, K_IOTA, K_ISA, K_ISS, K_T80, K_T81, K_EPS = 0, 128, 256, 304, 320, 321, 322, 323, 324
K_N = K_EPS + 2 * CW

T_REM, T_BIAS, TL = 2, 3, 4

OUT_AT = (0, 0, 3, 6, CW)

B_CONV, B_L1M, B_L1R, B_L2, B_FT, B_Y, B_YT = 0, 2, 4, 5, 6, 6, 7

LAST_STEP = NCHUNK + 6


class Chain:

    def __init__(self, eng, sem, per):
        self.eng, self.sem, self.per, self.n = eng, sem, per, 0

    def turn(self, i, n=0):
        self.base, self.n = i * self.per, n

    def count(self, ins):
        ins.then_inc(self.sem, 1)
        self.n += 1

    def wait(self):
        wait(self.eng, self.sem, self.base + self.n)

    def end(self):
        assert self.n == self.per, (self.n, self.per)


def known(i):
    return isinstance(i, int)


def wait(eng, sem, value):
    if not known(value) or value > 0:
        eng.wait_ge(sem, value)


def chunk_at(t, j, pair, lag):
    c = t - lag
    if known(c) and not 0 <= c < NCHUNK:
        return None
    behind = 1 if lag > j else 0
    return c, (j - lag) % CHUNKS, (pair + behind) % 2


def tile_at(t, j, s, lag):
    behind = (lag - s + GROUPS - 1) // GROUPS
    c = t - 4 - behind
    if known(c) and not 0 <= c < NCHUNK:
        return None
    s = (s - lag) % GROUPS
    return GROUPS * c + s, s, c, (j - 4 - behind) % CHUNKS


def run_steps(eng, step):
    for t in range(CHUNKS):
        step(t, t, 0)
    with eng.Fori(1, PAIRS) as pair:
        for j in range(CHUNKS):
            with eng.register(f"pair_{eng.engine.name}_{j}") as copy:
                eng.reg_mov(copy, pair)
                here = eng.snap(copy, min_val=1, max_val=PAIRS - 1)
                step(here * CHUNKS + j, j, here)
    for t in range(NCHUNK, LAST_STEP):
        step(t, t % CHUNKS, t // CHUNKS)


def build(nc, x_d, wa_d, ba_d, ws_d, bs_d, cst_d, out_d):
    with ExitStack() as ctx:
        def sb(name, shape, dt):
            return ctx.enter_context(nc.sbuf_tensor(name, shape, dt))

        def sem(name):
            return ctx.enter_context(nc.semaphore(name))

        xbuf = sb("xbuf", [P, 2 * C * W], F32)
        n32 = sb("n32", [P, 2, HALF, C], F32)
        nhi = sb("nhi", [P, RING, C], F16)
        nlo = sb("nlo", [P, RING, C], F16)
        cst = sb("consts", [P, K_N], F32)
        band = sb("band", [P, P], F16)
        identb = sb("identb", [P, P], BF16)
        stat = sb("stat", [P, 2 * CW, 3], F32)
        s_var = sb("s_var", [P, 2, 2 * CW], F32)
        s_sqrt = sb("s_sqrt", [P, 2, 2 * CW], F32)
        s_r0 = sb("s_r0", [P, 2 * CW], F32)
        s_nt = sb("s_nt", [P, 2 * CW], F32)
        s_nu = sb("s_nu", [P, 2 * CW], F32)
        mean = sb("mean", [P, 4, 2 * CW], F32)
        rstd = sb("rstd", [P, 4, 2 * CW], F32)
        rn = sb("rn", [P, 4, CW], F32)
        gain = sb("gain", [P, 4, CW], F32)
        shift = sb("shift", [P, 4, CW], F32)
        ut = sb("ut", [P, CW, UC], F32)
        u = sb("u", [P, CW, UC], F32)
        g = sb("g", [P, CW, 3 * NIB], F32)
        gw = sb("gw", [P, CW, 3, NIB], F32)
        mx1 = sb("mx1", [P, CW, 3], F32)
        nfree = sb("nfree", [P, CW, 3], F32)
        nhit = sb("nhit", [P, CW, 3], F32)
        marks = sb("marks", [P, CW, 3], F32)
        noadd = sb("noadd", [P, CW], F32)
        subraw = sb("subraw", [P, CW], F32)
        xres = sb("xres", [P, CW, 2], F32)
        msk = sb("msk", [P, 4, 3, CW], F32)
        val = sb("val", [P, CW, NV], BF16)
        feat = sb("feat", [P, 2, CW, P], BF16)
        featT = sb("featT", [P, 2, 2, 4 * P], BF16)
        h1m = sb("h1m", [P, 2, 512], F32)
        h1hi = sb("h1hi", [P, 2, 512], F32R)
        h1lo = sb("h1lo", [P, 2, 512], F32R)
        h2 = sb("h2", [P, 2 * GROUPS, 512], F32)
        ysb = sb("ysb", [P, 512], F32)
        ya = sb("ya", [P, CW, 2, 2], F32)
        ys = sb("ys", [P, CW, 2, 2], F32)
        yy = sb("yy", [P, CW, 2, 2], F32)
        yc = sb("yc", [P, CW, 2], F32)
        yr = sb("yr", [P, CW, 2], F32)
        yrr = sb("yrr", [P, CW, 2], F32)
        ycar = sb("ycar", [P, CW], F32)
        ycar2 = sb("ycar2", [P, CW], F32)
        hot = sb("hot", [P, CW, 2, NIB], F32)
        raw = h2[:, :, :].rearrange("p b n -> p (b n)")
        nat = raw[:, 0:2 * D].rearrange("p (k d) -> p k d", k=2)
        nat2, nat2r, nat3 = (raw[:, (2 + k) * P:(3 + k) * P] for k in range(3))
        tl = raw[:, 5 * P:5 * P + TL * P // 2].bitcast(BF16) \
            .rearrange("p (k n) -> p k n", k=TL)
        natb = sb("natb", [P, 2], F32)
        b2 = sb("b2", [P, 2], F32)
        base, res, res2 = (raw[:, k * P:k * P + 3 * NV].rearrange("p (k v) -> p k v", k=3) for k in (8, 9, 10))
        part = sb("part", [P, 3, PARTS, NV], BF16)
        w1 = sb("w1", [P, TL, P], BF16)
        w2m = sb("w2m", [P, P], F32)
        w2r = sb("w2r", [P, 2, P], F32R)
        w3 = sb("w3", [P, 32], F32)

        ps = ctx.enter_context(nc.psum_tensor("ps", [P, 8, 512], F32))
        ftp = ps[:, B_FT, :].bitcast(BF16)
        ytv = ps[:, B_YT, :].rearrange("p (b m o) -> p b m o", b=CW, m=2)

        cst_loaded = sem("cst_loaded")
        w_loaded = sem("w_loaded")
        zeroed = sem("zeroed")
        band_ready = sem("band_ready")
        setup_v = sem("setup_v")
        setup_pe = sem("setup_pe")
        first_loaded = sem("first_loaded")
        x_loaded = [sem(f"x_loaded{h}") for h in range(HALVES)]
        stored = [[sem(f"stored{h}_{i}") for i in range(len(RANGES))] for h in range(HALVES)]
        last_stored = sem("last_stored")
        ln = sem("ln")
        var_ready = sem("var_ready")
        sqrt_ready = sem("sqrt_ready")
        fin_ready = sem("fin_ready")
        n_ready = sem("n_ready")
        hi_ready = sem("hi_ready")
        lo_ready = sem("lo_ready")
        conv_done = sem("conv_done")
        x1_done = sem("x1_done")
        u_read = sem("u_read")
        dec = sem("dec")
        rank_ready = sem("rank_ready")
        top_ready = sem("top_ready")
        feat_ready = sem("feat_ready")
        ft_done = sem("ft_done")
        ft_copied = sem("ft_copied")
        l1m_done = sem("l1m_done")
        l1r_done = sem("l1r_done")
        h1m_ready = sem("h1m_ready")
        h1hi_ready = sem("h1hi_ready")
        h1lo_ready = sem("h1lo_ready")
        l2_done = sem("l2_done")
        h2_ready = sem("h2_ready")
        l3_done = sem("l3_done")
        y_copied = sem("y_copied")
        yt_done = sem("yt_done")
        y_read = sem("y_read")
        out_ready = sem("out_ready")
        hotc = sem("hotc")

        def xview(parity):
            lo = parity * (C * W)
            return xbuf[:, bass.ds(lo, C * W)].rearrange("p (c w) -> p w c", w=W)

        def over(ap, shape):
            return ap.broadcast_to(shape)

        block = ctx.enter_context(nc.Block())

        @block.sync
        def _(sp):
            def tile_part(parity, img, chans, cols):
                c0, c1 = chans
                return xbuf[img * H:(img + 1) * H, bass.ds(parity * (C * W) + c0 * W, (c1 - c0) * W)] \
                    .rearrange("p (c w) -> p c w", w=W)[:, :, cols[0]:cols[1]]

            def dram_part(ap, pair, img, chans, cols):
                return ap[bass.ds(pair * IMGS + img, 1), chans[0]:chans[1], :, cols[0]:cols[1]] \
                    .rearrange("b c h w -> (b h) c w")

            def load(pair, parity, chans, cols, loaded):
                for img in range(IMGS):
                    sp.dma_start(tile_part(parity, img, chans, cols), dram_part(x_d, pair, img, chans, cols)) \
                        .then_inc(loaded, 16)

            def store(pair, chans, cols, signal):
                for img in range(IMGS):
                    sp.dma_start(dram_part(out_d, pair, img, chans, cols),
                                 tile_part(pair % 2, img, chans, cols)).then_inc(signal, 16)

            def load_weights():
                sp.wait_ge(zeroed, 1)
                loads = [
                    (nat[0:D, 0, :], wa_d[0]), (nat[D:P, 0, :], ws_d[0, 0:MAIN]),
                    (nat2[0:D, 0:D], wa_d[1]), (nat2[0:D, D:P], ws_d[1, :, 0:MAIN]),
                    (natb[0:D, 0:1], ba_d[0].unsqueeze(1)), (natb[D:P, 0:1], bs_d[0, 0:MAIN].unsqueeze(1)),
                    (b2[0:D, 0:1], ba_d[1].unsqueeze(1)), (b2[0:D, 1:2], bs_d[1].unsqueeze(1)),
                ]
                for q in range(4):
                    rows = slice(REM * q, REM * (q + 1))
                    loads += [(nat[rows, 1, :], ws_d[0, MAIN:D]), (nat2r[0:D, rows], ws_d[1, :, MAIN:D]),
                              (natb[rows, 1:2], bs_d[0, MAIN:D].unsqueeze(1))]
                for i, (w_d, b_d, f) in enumerate(((wa_d, ba_d, RESULT), (wa_d, ba_d, CARRY_F),
                                                   (ws_d, bs_d, RESULT), (ws_d, bs_d, CARRY_F))):
                    at = D + i // 2
                    loads += [(nat3[i:i + 1, 0:D], w_d[2, f:f + 1]), (nat3[i:i + 1, at:at + 1], b_d[2:3, f:f + 1])]
                assert len(loads) == W_DMAS
                for dst, src in loads:
                    sp.dma_start(dst, src).then_inc(w_loaded, 16)

            sp.dma_start(cst[:, :], cst_d).then_inc(cst_loaded, 16)
            load(0, 0, (0, C), (0, FIRST_PART), first_loaded)
            load_weights()
            for pair in range(2):
                for h in range(HALVES):
                    if pair > 0:
                        sp.wait_ge(x_loaded[h], HALF_TILE * pair)
                    for chans in RANGES:
                        start = FIRST_PART if pair == 0 and h == 0 else h * HALF_W
                        load(pair, pair, chans, (start, (h + 1) * HALF_W), x_loaded[h])

            def leave(pair, i, h):
                cols = (h * HALF_W, (h + 1) * HALF_W)
                store(pair, RANGES[i], cols, stored[h][i])

            def enter(pair, i, h):
                sp.wait_ge(stored[h][i], 16 * IMGS * (pair + 1))
                load(pair + 2, pair % 2, RANGES[i], (h * HALF_W, (h + 1) * HALF_W), x_loaded[h])

            def chunks_by(pair, h):
                return pair * CHUNKS + (h + 1) * (CHUNKS // HALVES)

            late = len(EARLY)
            with sp.Fori(0, PAIRS - 2) as pair:
                for h in range(HALVES):
                    sp.wait_ge(x_loaded[h], HALF_TILE * (pair + 2))
                for h in range(HALVES):
                    sp.wait_ge(out_ready, chunks_by(pair, h))
                    for i in range(late):
                        leave(pair, i, h)
                    for i in range(late):
                        enter(pair, i, h)
                    sp.wait_ge(hotc, chunks_by(pair, h) * HOT_STEPS)
                    leave(pair, late, h)
                    enter(pair, late, h)
            pair = PAIRS - 2
            for h in range(HALVES):
                sp.wait_ge(out_ready, chunks_by(pair, h))
                for i in range(late):
                    leave(pair, i, h)
                sp.wait_ge(hotc, chunks_by(pair, h) * HOT_STEPS)
                leave(pair, late, h)
            pair = PAIRS - 1
            for cols in zip(LAST_PARTS, LAST_PARTS[1:]):
                chunks = pair * CHUNKS + cols[1] // CW
                sp.wait_ge(out_ready, chunks)
                for chans in EARLY:
                    store(pair, chans, cols, last_stored)
                sp.wait_ge(hotc, chunks * HOT_STEPS)
                store(pair, LATE, cols, last_stored)
            for h in range(HALVES):
                for i in range(len(RANGES)):
                    sp.wait_ge(stored[h][i], 16 * IMGS * (PAIRS - 1))
            sp.wait_ge(last_stored, 16 * IMGS * len(RANGES) * (len(LAST_PARTS) - 1))

        @block.vector
        def _(v):
            v.memset(nat2[:, :], 0.0)
            v.memset(nat2r[:, :], 0.0)
            v.memset(nat3[:, :], 0.0)
            v.memset(b2[:, :], 0.0)
            v.memset(base[:, :, :], 0.0).then_inc(zeroed, 1)
            v.memset(tl[:, :, :], 0.0)
            v.memset(feat[:, :, :, :], 0.0)
            v.memset(stat[:, :, :], 0.0)
            v.memset(val[:, :, V_ONE:V_ONE + 1], 1.0).then_inc(zeroed, 1)
            n_setup = [0]

            def done(ins):
                n_setup[0] += 1
                ins.then_inc(setup_v, 1)
                v.wait_ge(setup_v, n_setup[0])

            v.wait_ge(zeroed, 2)
            v.wait_ge(cst_loaded, 16)
            v.tensor_copy(identb[:, :], cst[:, K_ID:K_ID + P])
            v.tensor_copy(band[:, :], cst[:, K_BAND:K_BAND + P]).then_inc(band_ready, 1)

            def setup_parts():
                v.wait_ge(w_loaded, W_DMAS * 16)
                for k in range(2):
                    for j in range(PARTS):
                        v.tensor_copy(base[:, k, 2 * j:2 * j + 2], nat[:, k, OP_ADD_F:OP_ADD_F + 2])
                    for at in (V_LO, V_HI):
                        v.tensor_copy(base[:, k, at:at + 2], nat[:, k, 0:2])
                    v.tensor_copy(base[:, k, V_ONE:V_ONE + 1], natb[:, k:k + 1])
                done(v.tensor_copy(base[:, 2, 0:2], b2[:, :]))
                done(v.tensor_copy(part[:, :, 0, :], base[:, :, :]))
                done(v.tensor_tensor(res[:, :, :], base[:, :, :], part[:, :, 0, :], ALU.subtract))
                done(v.tensor_copy(part[:, :, 1, :], res[:, :, :]))
                done(v.tensor_tensor(res2[:, :, :], res[:, :, :], part[:, :, 1, :], ALU.subtract))
                done(v.tensor_copy(part[:, :, 2, :], res2[:, :, :]))
                flat = part[:, :, :, :].rearrange("p k j v -> p k (j v)")
                half = PARTS * NV
                for pos in range(2):
                    v.tensor_scalar(tl[:, pos, 0:half], flat[:, 0, :], cst[:, K_ISA:K_ISA + 1], None, ALU.mult)
                    v.tensor_scalar(tl[:, pos, half:2 * half], flat[:, 0, :], cst[:, K_ISS:K_ISS + 1], None, ALU.mult)
                v.tensor_copy(tl[:, T_REM, half:2 * half], flat[:, 1, :])
                for m in range(2):
                    for j in range(PARTS):
                        at = (m * PARTS + j) * NV + V_ONE
                        if j == 0:
                            one = K_T80 if m == 0 else K_T81
                            ins = v.tensor_tensor(tl[:, T_BIAS, at:at + 1], part[:, 2, j, m:m + 1], cst[:, one:one + 1],
                                                  ALU.add)
                        else:
                            ins = v.tensor_copy(tl[:, T_BIAS, at:at + 1], part[:, 2, j, m:m + 1])
                done(ins)
                for k, parts, at in ((0, slice(0, P), V_HI), (1, slice(0, P), V_LO),
                                     (T_REM, slice(0, P // 2), V_HI), (T_REM, slice(P // 2, P), V_LO)):
                    rows = tl[parts, k, 0:ROWS].rearrange("p (r v) -> p r v", v=NV)
                    ins = v.memset(rows[:, :, at:at + 2], 0.0)
                done(ins)

            def setup_weights():
                v.wait_ge(setup_pe, 1)
                v.tensor_copy(w1[:, :, :], ftp[:, 0:TL * P].rearrange("p (k n) -> p k n", k=TL))
                wt = ps[:, B_YT, :].rearrange("p (k n) -> p k n", k=4)
                v.tensor_copy(w2m[:, :], wt[:, 0, :])
                v.tensor_copy(w3[:, :], wt[:, 2, 0:32])
                for pos in range(2):
                    mine, other = (slice(k * P // 2, (k + 1) * P // 2) for k in (pos, 1 - pos))
                    v.tensor_scalar(w2r[other, pos, :], wt[other, 1, :], 0.0, None, ALU.mult)
                    ins = v.tensor_copy(w2r[mine, pos, :], wt[mine, 1, :])
                done(ins)
                for pos in range(2):
                    q = 2 * pos + 1
                    rows = slice(32 * q, 32 * q + 32)
                    ins = v.tensor_tensor(w2r[rows, pos, :], wt[rows, 1, :], w2r[rows, pos, :], ALU.subtract)
                done(ins)
                assert n_setup[0] == SETUP_V

            lnc = Chain(v, ln, LN_STEPS)
            hc = Chain(v, hotc, HOT_STEPS)
            four = [P, CW, 2, 2]
            hot_shape = [P, CW, 2, NIB]

            def variance(t, j):
                lnc.wait()
                wait(v, out_ready, t - 5)
                lnc.count(v.scalar_tensor_tensor(s_var[:, j % 2, :], stat[:, :, 2], 1.0 / C,
                                                 cst[:, K_EPS:K_EPS + 2 * CW], ALU.mult, ALU.add))
                v.tensor_copy(mean[:, j % 4, :], stat[:, :, 1])

            def sigma(i, t, j):
                k, b = (j - 1) % 4, (j - 1) % 2
                if i == 0:
                    lnc.turn(t - 1, AGG_STEPS)
                    v.wait_ge(sqrt_ready, t)
                    lnc.count(v.reciprocal(s_r0[:, :], s_sqrt[:, b, :]))
                    return
                lnc.wait()
                if i == 1:
                    lnc.count(v.scalar_tensor_tensor(s_nt[:, :], s_r0[:, :], -0.5, s_r0[:, :], ALU.mult, ALU.mult))
                elif i == 2:
                    lnc.count(v.tensor_tensor(s_nu[:, :], s_nt[:, :], s_var[:, b, :], ALU.mult))
                elif i == 3:
                    lnc.count(v.scalar_tensor_tensor(rstd[:, k, :], s_nu[:, :], 1.5, s_r0[:, :], ALU.add, ALU.mult))
                    lnc.end()
                else:
                    v.tensor_scalar(rn[:, k, :], rstd[:, k, 0:CW], SCALE / 9.0, None, ALU.mult)
                    v.tensor_scalar(gain[:, k, :], rstd[:, k, CW:], 1.0, None, ALU.add)
                    v.scalar_tensor_tensor(shift[:, k, :], mean[:, k, CW:], -1.0, rstd[:, k, CW:],
                                           ALU.mult, ALU.mult).then_inc(fin_ready, 1)

            def result(i, last, k):
                c, jc, par = last
                cols = xview(par)[:, jc * CW:(jc + 1) * CW, :]
                add, sub, act = (msk[:, k, n, :] for n in range(3))
                if i == 0:
                    hc.turn(c)
                    hc.wait()
                    v.wait_ge(feat_ready, c + 1)
                    v.wait_ge(yt_done, c + 1)
                    v.tensor_tensor(ya[:, :, :, :], ytv[:, :, :, 0:2],
                                    over(add.unsqueeze(2).unsqueeze(3), four), ALU.mult)
                    v.tensor_tensor(ys[:, :, :, :], ytv[:, :, :, 2:4],
                                    over(sub.unsqueeze(2).unsqueeze(3), four), ALU.mult).then_inc(y_read, 1)
                    return
                if i == 1:
                    v.wait_ge(y_read, c + 1)
                    hc.count(v.tensor_tensor(yy[:, :, :, :], ya[:, :, :, :], ys[:, :, :, :], ALU.add))
                    return
                hc.wait()
                if i == 2:
                    v.tensor_scalar(ycar[:, :], yy[:, :, 1, 1], 0.5, None, ALU.is_gt)
                    hc.count(v.tensor_scalar(yc[:, :, :], yy[:, :, :, 0], 0.0, float(NIB - 1), ALU.max, ALU.min))
                elif i == 3:
                    v.tensor_tensor(ycar2[:, :], ycar[:, :], act, ALU.mult)
                    hc.count(v.tensor_scalar(yr[:, :, :], yc[:, :, :], MAGIC, MAGIC, ALU.add, ALU.subtract))
                elif i == 4:
                    hc.count(v.scalar_tensor_tensor(yrr[:, :, :], yr[:, :, :], 1.0,
                                                    over(act.unsqueeze(2), [P, CW, 2]), ALU.add, ALU.mult))
                elif i == 5:
                    hc.count(v.tensor_tensor(hot[:, :, :, :],
                                             over(cst[:, K_IOTA:K_IOTA + NIB].unsqueeze(1).unsqueeze(2), hot_shape),
                                             over(yrr[:, :, :].unsqueeze(3), hot_shape), ALU.is_equal))
                elif i in (6, 7):
                    at = OUT_LO if i == 6 else OUT_HI
                    v.wait_ge(out_ready, c + 1)
                    hc.count(v.scalar_tensor_tensor(cols[:, :, at:at + NIB], hot[:, :, i - 6, :], 2.0,
                                                    cols[:, :, at:at + NIB], ALU.mult, ALU.add))
                else:
                    hc.count(v.tensor_tensor(cols[:, :, CARRY], cols[:, :, CARRY], ycar2[:, :], ALU.add))
                    hc.end()

            def step(t, j, pair):
                first = chunk_at(t, j, pair, 0)
                norm = chunk_at(t, j, pair, 1)
                conv = chunk_at(t, j, pair, 2)
                tok = chunk_at(t, j, pair, 3)
                last = chunk_at(t, j, pair, 6)
                ends = not known(t) or t <= NCHUNK + 1
                begins = not known(t) or 1 <= t <= NCHUNK + 2

                def finish(i):
                    if begins:
                        sigma(i, t, j)

                def put(i):
                    if last:
                        result(i, last, (j - 6) % 4)

                def normalise(w):
                    if norm:
                        c, jc, par = norm
                        if w == 0:
                            v.wait_ge(fin_ready, t)
                        if w % HALF == 0:
                            wait(v, lo_ready, 2 * c + w // HALF - 1)
                        k = (j - 1) % 4
                        ins = v.tensor_scalar(n32[:, w // HALF, w % HALF, :], xview(par)[:, jc * CW + w, :],
                                              mean[:, k, w:w + 1], rn[:, k, w:w + 1], ALU.subtract, ALU.mult)
                        if w % HALF == HALF - 1:
                            ins.then_inc(n_ready, 1)

                def statistics(chunk, at, s):
                    c, jc, par = chunk
                    w = jc * CW + 2 * s
                    return v.bn_stats(stat[:, at + 2 * s:at + 2 * s + 2, :].rearrange("p w n -> p (w n)"),
                                      xview(par)[:, w:w + 2, :].rearrange("p w c -> p c w"))

                def x_statistics(s):
                    if first:
                        return statistics(first, 0, s)

                def x1_statistics(s):
                    if conv:
                        return statistics(conv, CW, s)

                def add_convolution(s):
                    if conv:
                        c, jc, par = conv
                        w = jc * CW + 2 * s
                        pair_cols = xview(par)[:, w:w + 2, :]
                        v.wait_ge(conv_done, 4 * c + s + 1)
                        v.tensor_tensor(pair_cols, ps[:, B_CONV + s % 2, :].rearrange("p (w c) -> p w c", w=2),
                                        pair_cols, ALU.add).then_inc(x1_done, 1)

                def wait_x1(s):
                    if conv:
                        v.wait_ge(x1_done, 4 * conv[0] + s + 1)

                def low_parts(s):
                    tile = tile_at(t, j, s, 2)
                    if tile:
                        two, b = 2 * tile[2] + tile[1] // 2, tile[1] // 2
                        v.wait_ge(h1hi_ready, two + 1)
                        v.scalar_tensor_tensor(h1lo[:, b, :], ps[:, B_L1R, :], 0.0, h1hi[:, b, :],
                                               ALU.max, ALU.subtract).then_inc(h1lo_ready, 1)

                if known(t) and t == 2:
                    setup_parts()
                if known(t) and t == 3:
                    setup_weights()
                low_parts(0)
                finish(0)
                if known(t) and t == 0:
                    v.wait_ge(first_loaded, 16 * IMGS)
                elif first:
                    half = {(FIRST_PART // CW if known(t) else 0): 0, CHUNKS // HALVES: 1}.get(j)
                    if half is not None:
                        v.wait_ge(x_loaded[half], HALF_TILE * (pair + 1))
                add_convolution(0)
                finish(1)
                x_statistics(0)
                finish(2)
                finish(3)
                finish(4)
                x_statistics(1)
                for w in range(HALF - 1):
                    normalise(w)
                wait_x1(0)
                normalise(HALF - 1)

                x1_statistics(0)
                add_convolution(1)
                for w in range(HALF, CW):
                    put(w - HALF)
                    normalise(w)

                wait_x1(1)
                low_parts(2)
                x1_statistics(1)
                put(4)
                add_convolution(2)
                x_statistics(2)
                wait_x1(2)
                put(5)
                x1_statistics(2)
                if tok:
                    v.wait_ge(rank_ready, tok[0] + 1)
                    v.tensor_reduce(mx1[:, :, :], gw[:, :, :, :], mybir.AxisListType.X,
                                    ALU.max).then_inc(top_ready, 1)
                add_convolution(3)
                put(6)
                counted = x_statistics(3)
                wait_x1(3)
                put(7)
                counted = x1_statistics(3) or counted
                if ends:
                    lnc.turn(t)
                    lnc.count(counted)
                put(8)
                if ends:
                    variance(t, j)

            run_steps(v, step)

        @block.gpsimd
        def _(pool):
            dc = Chain(pool, dec, DEC_STEPS)

            def step(t, j, pair):
                norm = chunk_at(t, j, pair, 1)
                tok = chunk_at(t, j, pair, 3)
                k4 = (j - 3) % 4

                def low_parts(h):
                    c, jc, par = norm
                    at = (jc * CW + h * HALF) % RING
                    pool.wait_ge(hi_ready, 2 * c + h + 1)
                    pool.tensor_tensor(nlo[:, at:at + HALF, :], n32[:, h, :, :], nhi[:, at:at + HALF, :],
                                       ALU.subtract).then_inc(lo_ready, 1)

                if tok:
                    c, jc, par = tok
                    dc.turn(c)
                    dc.wait()
                    pool.wait_ge(fin_ready, t)
                    shape = [P, CW, UC]
                    dc.count(pool.tensor_tensor(ut[:, :, :], xview(par)[:, jc * CW:(jc + 1) * CW, 0:UC],
                                               over(mean[:, (j - 1) % 4, CW:].unsqueeze(2), shape), ALU.subtract))
                    dc.wait()
                    pool.tensor_tensor(u[:, :, :], ut[:, :, :],
                                       over(rstd[:, (j - 1) % 4, CW:].unsqueeze(2), shape),
                                       ALU.mult).then_inc(u_read, 1)
                    pool.wait_ge(u_read, c + 1)
                    wait(pool, hotc, (c - 3) * HOT_STEPS)
                if norm:
                    low_parts(0)
                if tok:
                    if known(c) and c == 0:
                        pool.wait_ge(zeroed, 2)
                        pool.wait_ge(cst_loaded, 16)
                    add, sub, act = (msk[:, k4, i, :] for i in range(3))
                    pool.tensor_scalar(g[:, :, :], u[:, :, ALU_LO:ALU_LO + 3 * NIB], 0.5, None, ALU.is_gt)
                    pool.tensor_scalar(marks[:, :, :], u[:, :, 0:3], 0.5, None, ALU.is_gt)
                    dc.count(pool.tensor_copy(val[:, :, 0:2], u[:, :, OP_COL:OP_COL + 2]))
                    dc.wait()
                    rank = cst[:, K_RANK:K_RANK + 3 * NIB]
                    pool.tensor_tensor(gw[:, :, :, :].rearrange("p b k n -> p b (k n)"), g[:, :, :],
                                       over(rank.unsqueeze(1), [P, CW, 3 * NIB]), ALU.mult).then_inc(rank_ready, 1)
                    pool.tensor_tensor(add, marks[:, :, 0], marks[:, :, 1], ALU.mult)
                    pool.tensor_tensor(subraw[:, :], marks[:, :, 0], marks[:, :, 2], ALU.mult)
                    pool.tensor_scalar(noadd[:, :], marks[:, :, 1], -1.0, 1.0, ALU.mult, ALU.add)
                    dc.count(pool.tensor_tensor(xres[:, :, :], u[:, :, OP_COL:OP_COL + 2], val[:, :, 0:2],
                                               ALU.subtract))
                    dc.wait()
                    pool.tensor_tensor(sub, subraw[:, :], noadd[:, :], ALU.mult)
                    dc.count(pool.tensor_copy(val[:, :, 2:4], xres[:, :, :]))
                    dc.wait()
                    pool.tensor_tensor(act, add, sub, ALU.add)
                    dc.count(pool.tensor_tensor(val[:, :, 4:6], xres[:, :, :], val[:, :, 2:4], ALU.subtract))
                if norm:
                    low_parts(1)
                if tok:
                    c = tok[0]
                    pool.wait_ge(top_ready, c + 1)
                    pool.tensor_tensor(nfree[:, :, :], over(rank[:, 0:1].unsqueeze(1), [P, CW, 3]), mx1[:, :, :],
                                       ALU.subtract)
                    dc.count(pool.tensor_scalar(nhit[:, :, :], mx1[:, :, :], 0.5, None, ALU.is_gt))
                    dc.wait()
                    pool.tensor_tensor(val[:, :, V_LO:V_LO + 2], nfree[:, :, 0:3:2], nhit[:, :, 0:3:2], ALU.mult)
                    dc.count(pool.tensor_tensor(val[:, :, V_HI:V_HI + 2],
                                               over(nfree[:, :, 1:2], [P, CW, 2]),
                                               over(nhit[:, :, 1:2], [P, CW, 2]), ALU.mult))
                    dc.wait()
                    wait(pool, ft_done, c - 1)
                    half = PARTS * NV
                    shape = [P, CW, PARTS, NV]
                    for m, mask in enumerate((add, sub)):
                        ins = pool.tensor_tensor(
                            feat[:, (j + 1) % 2, :, m * half:(m + 1) * half].rearrange("p b (j v) -> p b j v", v=NV),
                            over(val[:, :, :].unsqueeze(2), shape), over(mask.unsqueeze(2).unsqueeze(3), shape),
                            ALU.mult)
                    ins.then_inc(feat_ready, 1)
                    dc.end()
                    pool.wait_ge(feat_ready, c + 1)

            run_steps(pool, step)

        @block.scalar
        def _(act):
            def step(t, j, pair):
                norm = chunk_at(t, j, pair, 1)
                tok = chunk_at(t, j, pair, 3)
                ffn = chunk_at(t, j, pair, 4)
                back = chunk_at(t, j, pair, 5)
                for s in range(GROUPS):
                    tile = tile_at(t, j, s, 1)
                    if tile:
                        tau = tile[0]
                        if tile[1] % 2 == 0:
                            act.wait_ge(l1r_done, 2 * tile[2] + tile[1] // 2 + 1)
                            wait(act, l2_done, tau - 2)
                            act.activation(h1hi[:, tile[1] // 2, :], ps[:, B_L1R, :],
                                           ACT.Relu).then_inc(h1hi_ready, 1)
                        act.wait_ge(l1m_done, tau + 1)
                        wait(act, l2_done, tau - 1)
                        act.activation(h1m[:, tile[1] % 2, :], ps[:, B_L1M + tile[1] % 2, :],
                                       ACT.Relu).then_inc(h1m_ready, 1)
                    tile = tile_at(t, j, s, 2)
                    if tile:
                        tau, i, c, jc = tile
                        act.wait_ge(l2_done, tau + 1)
                        wait(act, l3_done, c - 1)
                        act.activation(h2[:, GROUPS * (jc % 2) + i, :], ps[:, B_L2, :],
                                       ACT.Relu).then_inc(h2_ready, 1)
                    if s == 0 and ffn:
                        c, jc, par = ffn
                        act.wait_ge(ft_done, c + 1)
                        wait(act, l2_done, 4 * c - 4)
                        act.activation(featT[:, jc % 2, :, :].rearrange("p a n -> p (a n)"), ftp,
                                       ACT.Copy).then_inc(ft_copied, 1)
                    if norm and s < 2:
                        c, jc, par = norm
                        at = (jc * CW + s * HALF) % RING
                        act.wait_ge(n_ready, 2 * c + s + 1)
                        wait(act, conv_done, 2 * (2 * c + s) - 5)
                        act.activation(nhi[:, at:at + HALF, :], n32[:, s, :, :], ACT.Copy).then_inc(hi_ready, 1)
                    if s == 3 and (not known(t) or t <= NCHUNK + 1):
                        act.wait_ge(ln, LN_STEPS * t + AGG_STEPS)
                        act.activation(s_sqrt[:, j % 2, :], s_var[:, j % 2, :], ACT.Sqrt).then_inc(sqrt_ready, 1)
                    if s == 3 and back:
                        c = back[0]
                        act.wait_ge(l3_done, c + 1)
                        wait(act, yt_done, c)
                        act.activation(ysb[:, :], ps[:, B_Y, :], ACT.Copy).then_inc(y_copied, 1)
                    if tok:
                        c, jc, par = tok
                        if s == 1:
                            act.wait_ge(u_read, c + 1)
                        k = (j - 1) % 4
                        for w in range(*OUT_AT[s:s + 2]):
                            col = xview(par)[:, jc * CW + w, :]
                            ins = act.activation(col, col, ACT.Identity, bias=shift[:, k, w:w + 1],
                                                 scale=gain[:, k, w:w + 1])
                        if s == 3:
                            ins.then_inc(out_ready, 1)

            run_steps(act, step)

        @block.tensor
        def _(pe):
            pe.wait_ge(band_ready, 1)
            ident = cst[:, K_ID:K_ID + P]

            def setup_weights():
                pe.wait_ge(setup_v, SETUP_V - 2)
                for k in range(TL):
                    pe.transpose(ftp[:, k * P:(k + 1) * P], tl[:, k, :], identb[:, :])
                for k, src in enumerate((nat2, nat2r, nat3)):
                    ins = pe.transpose(ps[:, B_YT, k * P:(k + 1) * P], src[:, :], ident)
                ins.then_inc(setup_pe, 1)

            def convolve(conv, s):
                c, jc, par = conv
                w = jc * CW + 2 * s
                bank = ps[:, B_CONV + s % 2, :].rearrange("p (w c) -> p w c", w=2)
                pieces = []
                for d in (0, -1, 1):
                    if 0 <= w + d and w + d + 2 <= W and (w + d) % RING != RING - 1:
                        pieces.append((0, 2, (w + d) % RING))
                    else:
                        pieces += [(i, 1, (w + d + i) % RING) for i in range(2) if 0 <= w + d + i < W]
                wait(pe, x1_done, 4 * c + s - 1)
                if s in (0, 1, 3):
                    pe.wait_ge(lo_ready, 2 * c + (1 if s == 0 else 2 if s == 1 or jc == CHUNKS - 1 else 3))
                n = 0
                for src in (nhi, nlo):
                    for i, k, at in pieces:
                        n += 1
                        ins = pe.matmul(bank[:, i:i + k, :], band[:, :], src[:, at:at + k, :],
                                        start=n == 1, stop=n == 2 * len(pieces))
                ins.then_inc(conv_done, 1)

            def step(t, j, pair):
                conv = chunk_at(t, j, pair, 2)
                ffn = chunk_at(t, j, pair, 4)
                back = chunk_at(t, j, pair, 5)
                last = chunk_at(t, j, pair, 6)
                if known(t) and t == 2:
                    setup_weights()
                if known(t) and t == 4:
                    pe.wait_ge(setup_v, SETUP_V)
                for s in range(GROUPS):
                    if conv:
                        convolve(conv, s)
                    tile = tile_at(t, j, s, 1)
                    if tile:
                        tau, i, c, jc = tile
                        if i == 0:
                            pe.wait_ge(ft_copied, c + 1)
                        rhs = featT[:, jc % 2, i // 2, :]
                        if i % 2 == 0:
                            wait(pe, h1lo_ready, 2 * c + i // 2)
                            pe.matmul(ps[:, B_L1R, :], w1[:, T_REM, :], rhs, start=True,
                                      stop=True).then_inc(l1r_done, 1)
                        wait(pe, h1m_ready, tau - 1)
                        pe.matmul(ps[:, B_L1M + i % 2, :], w1[:, i % 2, :], rhs, start=True,
                                  stop=True).then_inc(l1m_done, 1)
                    tile = tile_at(t, j, s, 2)
                    if tile:
                        tau, i, c, jc = tile
                        pe.wait_ge(h1m_ready, tau + 1)
                        wait(pe, h2_ready, tau)
                        pe.matmul(ps[:, B_L2, :], w1[:, T_BIAS, :], featT[:, jc % 2, i // 2, :], start=True,
                                  stop=False)
                        pe.matmul(ps[:, B_L2, :], w2m[:, :], h1m[:, i % 2, :], start=False, stop=False)
                        pe.matmul(ps[:, B_L2, :], w2r[:, i % 2, :], h1hi[:, i // 2, :], start=False, stop=False)
                        pe.wait_ge(h1lo_ready, 2 * c + i // 2 + 1)
                        pe.matmul(ps[:, B_L2, :], w2r[:, i % 2, :], h1lo[:, i // 2, :], start=False,
                                  stop=True).then_inc(l2_done, 1)
                    if s == 2 and back:
                        c, jc, par = back
                        pe.wait_ge(h2_ready, 4 * c + 4)
                        for i in range(GROUPS):
                            ins = pe.matmul(ps[32 * i:32 * i + 32, B_Y, :], w3[:, :],
                                            h2[:, GROUPS * (jc % 2) + i, :], start=True, stop=True)
                        ins.then_inc(l3_done, 1)
                    if s == 0 and last:
                        c = last[0]
                        pe.wait_ge(y_copied, c + 1)
                        wait(pe, y_read, c)
                        for q in range(4):
                            ins = pe.transpose(ps[:, B_YT, q * P:(q + 1) * P], ysb[:, q * P:(q + 1) * P], ident)
                        ins.then_inc(yt_done, 1)
                    if s == 0 and ffn:
                        c, jc, par = ffn
                        pe.wait_ge(feat_ready, c + 1)
                        wait(pe, y_copied, c - 1)
                        for b in range(CW):
                            at = (b % 2) * 4 * P + b // 2 * P
                            ins = pe.transpose(ftp[:, at:at + P], feat[:, jc % 2, b, :], identb[:, :])
                        ins.then_inc(ft_done, 1)

            run_steps(pe, step)


W_DMAS = 8 + 12 + 8
HALF_TILE = 16 * IMGS * len(RANGES)
SETUP_V = 10
AGG_STEPS, LN_STEPS = 2, 6
HOT_STEPS = 8
DEC_STEPS = 7


def constants():
    import numpy as np

    k = np.zeros((P, K_N), np.float32)
    k[:, K_ID:K_ID + P] = np.eye(P)
    rows = np.arange(P)
    near = (np.abs(rows[:, None] - rows[None, :]) <= 1) & (rows[:, None] // H == rows[None, :] // H)
    k[:, K_BAND:K_BAND + P] = near / SCALE
    k[:, K_RANK:K_RANK + 3 * NIB] = np.tile(NIB - np.arange(NIB), 3)
    k[:, K_IOTA:K_IOTA + NIB] = np.arange(NIB) + 1
    k[:, K_ISA] = rows < D
    k[:, K_ISS] = rows >= D
    k[:, K_T80] = rows == D
    k[:, K_T81] = rows == D + 1
    k[:, K_EPS:K_EPS + CW] = 1e-6
    k[:, K_EPS + CW:] = 1e-5
    return k


def kernel(x, L0_ffn_Wa, L0_ffn_ba, L0_ffn_Ws, L0_ffn_bs):
    import numpy as np
    import concourse.bacc as bacc
    from concourse.bass_utils import run_bass_kernel_spmd

    nc = bacc.Bacc("TRN2", target_bir_lowering=False, num_devices=1)
    arrays = {"x": x, "wa": L0_ffn_Wa, "ba": L0_ffn_ba, "ws": L0_ffn_Ws, "bs": L0_ffn_bs, "cst": constants()}
    arrays = {k: np.ascontiguousarray(a) for k, a in arrays.items()}
    aps = [nc.dram_tensor(k, a.shape, mybir.dt.from_np(a.dtype), kind="ExternalInput").ap()
           for k, a in arrays.items()]
    out = nc.dram_tensor("out", (B, C, H, W), F32, kind="ExternalOutput").ap()
    build(nc, *aps, out)
    r = run_bass_kernel_spmd(nc, [arrays], core_ids=[0])
    return r.results[0]["out"]
```
